# Optimizing a Trainium2 kernel written in Bass

```python
import numpy as np
import jax
import jax.numpy as jnp

def _softmax(x, axis=-1):
    return jax.nn.softmax(x, axis=axis)

def _gelu(x):
    return jax.nn.gelu(x, approximate=True)

def _silu(x):
    return jax.nn.silu(x)

def _sigmoid(x):
    return jax.nn.sigmoid(x)

def _layernorm(x, axis=-1, eps=1e-05):
    m = jnp.mean(x, axis=axis, keepdims=True)
    v = jnp.var(x, axis=axis, keepdims=True)
    return (x - m) / jnp.sqrt(v + eps)

def _scatter_add(tgt, idx, src, axis=0):
    return tgt.at[idx].add(src)

def _segment_sum(src, seg, n):
    return jax.ops.segment_sum(src, seg, n)
kernel_name = 'mk_decoder_postln_d2_seqx_r8_766bea'

def setup_inputs(seed: int=0):
    np.random.seed(seed)
    _w = jnp.asarray

    def _rec_inputs():
        import jax
        import jax.numpy as jnp
        _rk = jax.random.key(seed)
        x = -0.000125 + 0.9999 * jax.random.normal(jax.random.fold_in(_rk, 1), (2, 256, 128), jnp.float32)
        _lenS = 256 - jax.random.randint(jax.random.fold_in(_rk, 7), (2,), 0, max(1, 256 // 4) + 1, jnp.int32)
        _lenS2 = 512 - jax.random.randint(jax.random.fold_in(_rk, 8), (2,), 0, max(1, 512 // 4) + 1, jnp.int32)
        _ctx_1024P = jax.random.normal(jax.random.fold_in(_rk, 11), (2, 16, 128), jnp.float32)
        _ctx_1024c = jax.random.dirichlet(jax.random.fold_in(_rk, 511), 0.3 * jnp.ones((16,), jnp.float32), (2, 512))
        _ctx_1024t = jnp.einsum('bsk,bkd->bsd', _ctx_1024c, _ctx_1024P)
        _ctx_1024t = _ctx_1024t * jax.lax.rsqrt(jnp.mean(jnp.square(_ctx_1024t)) + 1e-12) * 0.953939
        ctx_1024 = -0.000514642 + 1.00011 * (_ctx_1024t + 0.3 * jax.random.normal(jax.random.fold_in(_rk, 611), (2, 512, 128), jnp.float32))
        _validS = jnp.arange(256)[None, :] < _lenS[:, None]
        _validS2 = jnp.arange(512)[None, :] < _lenS2[:, None]
        _causal = jnp.tril(jnp.ones((256, 256), dtype=bool))
        mask_BxS2_bf1 = jnp.ones((2, 512), dtype=bool)
        mask_BxS2_bk0 = jnp.logical_not(jnp.broadcast_to(_validS2[:, :], (2, 512)))
        return (x, ctx_1024, mask_BxS2_bf1, mask_BxS2_bk0)
    x, ctx_1024, mask_BxS2_bf1, mask_BxS2_bk0 = _rec_inputs()

    def _L0_attn_setup():
        import jax, jax.numpy as jnp
        import numpy as np
        import math
        H = 16
        LORA_SCALING = 16 / 8
        NEG_INF = -1e+30

        def _alibi_slopes(n_heads):
            start = 2.0 ** (-2.0 ** (-(math.log2(n_heads) - 3)))
            return jnp.asarray([start * start ** i for i in range(n_heads)], dtype=jnp.float32)

        def _lora(x, W, A, Bm):
            return x @ W.T + x @ Bm.T @ A.T * LORA_SCALING
        key = jax.random.key(seed)
        ks = jax.random.split(key, 11)
        B, T, E, r = (4, 256, 128, 8)
        d = {'x': jax.random.normal(ks[0], (B, T, E), jnp.float32), 'Wq': jax.random.normal(ks[1], (E, E), jnp.float32) * E ** (-0.5), 'Aq': jax.random.normal(ks[2], (E, r), jnp.float32) * 0.01, 'Bq': jax.random.normal(ks[3], (r, E), jnp.float32) * 0.01, 'Wk': jax.random.normal(ks[4], (E, E), jnp.float32) * E ** (-0.5), 'Ak': jax.random.normal(ks[5], (E, r), jnp.float32) * 0.01, 'Bk': jax.random.normal(ks[6], (r, E), jnp.float32) * 0.01, 'Wv': jax.random.normal(ks[7], (E, E), jnp.float32) * E ** (-0.5), 'Av': jax.random.normal(ks[8], (E, r), jnp.float32) * 0.01, 'Bv': jax.random.normal(ks[9], (r, E), jnp.float32) * 0.01, 'Wp': jax.random.normal(ks[10], (E, E), jnp.float32) * E ** (-0.5)}
        return d
    _L0_attn_all = _L0_attn_setup()
    _L0_attn_in = {k: v for k, v in _L0_attn_all.items() if k in ('Wq', 'Aq', 'Bq', 'Wk', 'Ak', 'Bk', 'Wv', 'Av', 'Bv', 'Wp')}
    del _L0_attn_all

    def _L0_xattn_setup():
        import jax, jax.numpy as jnp
        import numpy as np
        EPS = 1e-06
        NUM_HEADS = 16
        DIM_HEADS = 64

        def _ln(x, scale, bias):
            mu = jnp.mean(x, axis=-1, keepdims=True)
            var = jnp.mean(jnp.square(x - mu), axis=-1, keepdims=True)
            return (x - mu) * jax.lax.rsqrt(var + EPS) * scale + bias
        key = jax.random.key(seed)
        ks = jax.random.split(key, 8)
        b, n, m, dim, ctx_dim = (8, 512, 32, 128, 128)
        inner = NUM_HEADS * DIM_HEADS
        x = jax.random.normal(ks[0], (b, n, dim), dtype=jnp.float32)
        context = jax.random.normal(ks[1], (b, m, ctx_dim), dtype=jnp.float32)
        mask = jnp.ones((b, m), dtype=bool)
        Wq = jax.random.normal(ks[2], (dim, inner), dtype=jnp.float32) / np.sqrt(dim)
        Wkv = jax.random.normal(ks[3], (ctx_dim, 2 * inner), dtype=jnp.float32) / np.sqrt(ctx_dim)
        null_kv = jax.random.normal(ks[4], (2, DIM_HEADS), dtype=jnp.float32)
        Wo = jax.random.normal(ks[5], (inner, dim), dtype=jnp.float32) / np.sqrt(inner)
        return {'x': x, 'context': context, 'mask': mask, 'ln1_s': jnp.ones((dim,), jnp.float32), 'ln1_b': jnp.zeros((dim,), jnp.float32), 'lnc_s': jnp.ones((ctx_dim,), jnp.float32), 'lnc_b': jnp.zeros((ctx_dim,), jnp.float32), 'Wq': Wq, 'Wkv': Wkv, 'null_kv': null_kv, 'Wo': Wo, 'lno_s': jnp.ones((dim,), jnp.float32), 'lno_b': jnp.zeros((dim,), jnp.float32)}
    _L0_xattn_all = _L0_xattn_setup()
    _L0_xattn_in = {k: v for k, v in _L0_xattn_all.items() if k in ('ln1_s', 'ln1_b', 'lnc_s', 'lnc_b', 'Wq', 'Wkv', 'null_kv', 'Wo', 'lno_s', 'lno_b')}
    del _L0_xattn_all

    def _L0_ffn_setup():
        import jax, jax.numpy as jnp
        import numpy as np
        DIM = 128
        NUM_EXPERTS = 8
        ACTIVE_EXPERTS = 2
        EXPERT_DIM = 256
        key = jax.random.key(seed)
        k1, k2, k3, k4 = jax.random.split(key, 4)
        x = jax.random.normal(k1, (1, 256, DIM), dtype=jnp.float32)
        gate_w = jax.random.normal(k2, (NUM_EXPERTS, DIM), dtype=jnp.float32) * 0.02
        balance_bias = jnp.zeros((NUM_EXPERTS,), dtype=jnp.float32)
        w1 = jax.random.normal(k3, (NUM_EXPERTS, EXPERT_DIM, DIM), dtype=jnp.float32) * 0.02
        w2 = jax.random.normal(k4, (NUM_EXPERTS, DIM, EXPERT_DIM), dtype=jnp.float32) * 0.02
        return {'x': x, 'gate_w': gate_w, 'balance_bias': balance_bias, 'w1': w1, 'w2': w2}
    _L0_ffn_all = _L0_ffn_setup()
    _L0_ffn_in = {k: v for k, v in _L0_ffn_all.items() if k in ('gate_w', 'balance_bias', 'w1', 'w2')}
    del _L0_ffn_all

    def _L1_attn_setup():
        import jax, jax.numpy as jnp
        import numpy as np
        import math
        WINDOW = 64
        N_HEAD = 16
        key = jax.random.key(seed)
        ks = jax.random.split(key, 5)
        B, L, D = (2, 512, 128)
        s = 0.02
        return {'x': jax.random.normal(ks[0], (B, L, D), dtype=jnp.float32), 'Wq': jax.random.normal(ks[1], (D, D), dtype=jnp.float32) * s, 'bq': jnp.zeros((D,), jnp.float32), 'Wk': jax.random.normal(ks[2], (D, D), dtype=jnp.float32) * s, 'bk': jnp.zeros((D,), jnp.float32), 'Wv': jax.random.normal(ks[3], (D, D), dtype=jnp.float32) * s, 'bv': jnp.zeros((D,), jnp.float32), 'Wo': jax.random.normal(ks[4], (D, D), dtype=jnp.float32) * s, 'bo': jnp.zeros((D,), jnp.float32)}
    _L1_attn_all = _L1_attn_setup()
    _L1_attn_in = {k: v for k, v in _L1_attn_all.items() if k in ('Wq', 'bq', 'Wk', 'bk', 'Wv', 'bv', 'Wo', 'bo')}
    del _L1_attn_all

    def _L1_xattn_setup():
        import jax, jax.numpy as jnp
        import numpy as np
        D_MODEL = 128
        N_HEADS = 16
        HEAD_DIM = D_MODEL // N_HEADS
        B, S = (4, 256)
        key = jax.random.key(seed)
        ks = jax.random.split(key, 12)
        s = 0.02
        q_input = jax.random.normal(ks[0], (B, S, D_MODEL), jnp.float32)
        k_input = jax.random.normal(ks[1], (B, S, D_MODEL), jnp.float32)
        v_input = jax.random.normal(ks[2], (B, S, D_MODEL), jnp.float32)
        valid_len = jax.random.randint(ks[3], (B, 1), S // 2, S + 1)
        key_padding_mask = jnp.arange(S)[None, :] >= valid_len
        Wq = jax.random.normal(ks[4], (D_MODEL, D_MODEL), jnp.float32) * s
        Wk = jax.random.normal(ks[5], (D_MODEL, D_MODEL), jnp.float32) * s
        Wv = jax.random.normal(ks[6], (D_MODEL, D_MODEL), jnp.float32) * s
        Wo = jax.random.normal(ks[7], (D_MODEL, D_MODEL), jnp.float32) * s
        bq = jnp.zeros((D_MODEL,), jnp.float32)
        bk = jnp.zeros((D_MODEL,), jnp.float32)
        bv = jnp.zeros((D_MODEL,), jnp.float32)
        bo = jnp.zeros((D_MODEL,), jnp.float32)
        return dict(q_input=q_input, k_input=k_input, v_input=v_input, key_padding_mask=key_padding_mask, Wq=Wq, bq=bq, Wk=Wk, bk=bk, Wv=Wv, bv=bv, Wo=Wo, bo=bo)
    _L1_xattn_all = _L1_xattn_setup()
    _L1_xattn_in = {k: v for k, v in _L1_xattn_all.items() if k in ('Wq', 'bq', 'Wk', 'bk', 'Wv', 'bv', 'Wo', 'bo')}
    del _L1_xattn_all

    def _L1_ffn_setup():
        import jax, jax.numpy as jnp
        import numpy as np
        E = 64
        K = 6
        CAP = 64
        ROUTE_SCALE = 1.0
        key = jax.random.key(seed)
        ks = jax.random.split(key, 9)
        B, S, D, I = (2, 128, 128, 88)
        SI = 2 * I
        s = 0.02
        return {'x': jax.random.normal(ks[0], (B, S, D), jnp.float32), 'gate_w': jax.random.normal(ks[1], (E, D), jnp.float32) * s, 'gate_b': jnp.zeros((E,), jnp.float32), 'w1': jax.random.normal(ks[2], (E, I, D), jnp.float32) * s, 'w2': jax.random.normal(ks[3], (E, D, I), jnp.float32) * s, 'w3': jax.random.normal(ks[4], (E, I, D), jnp.float32) * s, 'ws1': jax.random.normal(ks[5], (SI, D), jnp.float32) * s, 'ws2': jax.random.normal(ks[6], (D, SI), jnp.float32) * s, 'ws3': jax.random.normal(ks[7], (SI, D), jnp.float32) * s}
    _L1_ffn_all = _L1_ffn_setup()
    _L1_ffn_in = {k: v for k, v in _L1_ffn_all.items() if k in ('gate_w', 'gate_b', 'w1', 'w2', 'w3', 'ws1', 'ws2', 'ws3')}
    del _L1_ffn_all
    return {'x': x, 'ctx_1024': ctx_1024, 'mask_BxS2_bf1': mask_BxS2_bf1, 'mask_BxS2_bk0': mask_BxS2_bk0, 'L0_attn_Wq': _L0_attn_in['Wq'], 'L0_attn_Aq': _L0_attn_in['Aq'], 'L0_attn_Bq': _L0_attn_in['Bq'], 'L0_attn_Wk': _L0_attn_in['Wk'], 'L0_attn_Ak': _L0_attn_in['Ak'], 'L0_attn_Bk': _L0_attn_in['Bk'], 'L0_attn_Wv': _L0_attn_in['Wv'], 'L0_attn_Av': _L0_attn_in['Av'], 'L0_attn_Bv': _L0_attn_in['Bv'], 'L0_attn_Wp': _L0_attn_in['Wp'], 'L0_xattn_ln1_s': _L0_xattn_in['ln1_s'], 'L0_xattn_ln1_b': _L0_xattn_in['ln1_b'], 'L0_xattn_lnc_s': _L0_xattn_in['lnc_s'], 'L0_xattn_lnc_b': _L0_xattn_in['lnc_b'], 'L0_xattn_Wq': _L0_xattn_in['Wq'], 'L0_xattn_Wkv': _L0_xattn_in['Wkv'], 'L0_xattn_null_kv': _L0_xattn_in['null_kv'], 'L0_xattn_Wo': _L0_xattn_in['Wo'], 'L0_xattn_lno_s': _L0_xattn_in['lno_s'], 'L0_xattn_lno_b': _L0_xattn_in['lno_b'], 'L0_ffn_gate_w': _L0_ffn_in['gate_w'], 'L0_ffn_balance_bias': _L0_ffn_in['balance_bias'], 'L0_ffn_w1': _L0_ffn_in['w1'], 'L0_ffn_w2': _L0_ffn_in['w2'], 'L1_attn_Wq': _L1_attn_in['Wq'], 'L1_attn_bq': _L1_attn_in['bq'], 'L1_attn_Wk': _L1_attn_in['Wk'], 'L1_attn_bk': _L1_attn_in['bk'], 'L1_attn_Wv': _L1_attn_in['Wv'], 'L1_attn_bv': _L1_attn_in['bv'], 'L1_attn_Wo': _L1_attn_in['Wo'], 'L1_attn_bo': _L1_attn_in['bo'], 'L1_xattn_Wq': _L1_xattn_in['Wq'], 'L1_xattn_bq': _L1_xattn_in['bq'], 'L1_xattn_Wk': _L1_xattn_in['Wk'], 'L1_xattn_bk': _L1_xattn_in['bk'], 'L1_xattn_Wv': _L1_xattn_in['Wv'], 'L1_xattn_bv': _L1_xattn_in['bv'], 'L1_xattn_Wo': _L1_xattn_in['Wo'], 'L1_xattn_bo': _L1_xattn_in['bo'], 'L1_ffn_gate_w': _L1_ffn_in['gate_w'], 'L1_ffn_gate_b': _L1_ffn_in['gate_b'], 'L1_ffn_w1': _L1_ffn_in['w1'], 'L1_ffn_w2': _L1_ffn_in['w2'], 'L1_ffn_w3': _L1_ffn_in['w3'], 'L1_ffn_ws1': _L1_ffn_in['ws1'], 'L1_ffn_ws2': _L1_ffn_in['ws2'], 'L1_ffn_ws3': _L1_ffn_in['ws3']}

def reference(x, ctx_1024, mask_BxS2_bf1, mask_BxS2_bk0, L0_attn_Wq, L0_attn_Aq, L0_attn_Bq, L0_attn_Wk, L0_attn_Ak, L0_attn_Bk, L0_attn_Wv, L0_attn_Av, L0_attn_Bv, L0_attn_Wp, L0_xattn_ln1_s, L0_xattn_ln1_b, L0_xattn_lnc_s, L0_xattn_lnc_b, L0_xattn_Wq, L0_xattn_Wkv, L0_xattn_null_kv, L0_xattn_Wo, L0_xattn_lno_s, L0_xattn_lno_b, L0_ffn_gate_w, L0_ffn_balance_bias, L0_ffn_w1, L0_ffn_w2, L1_attn_Wq, L1_attn_bq, L1_attn_Wk, L1_attn_bk, L1_attn_Wv, L1_attn_bv, L1_attn_Wo, L1_attn_bo, L1_xattn_Wq, L1_xattn_bq, L1_xattn_Wk, L1_xattn_bk, L1_xattn_Wv, L1_xattn_bv, L1_xattn_Wo, L1_xattn_bo, L1_ffn_gate_w, L1_ffn_gate_b, L1_ffn_w1, L1_ffn_w2, L1_ffn_w3, L1_ffn_ws1, L1_ffn_ws2, L1_ffn_ws3):
    import jax
    import jax.numpy as jnp

    def _L0_attn_ref(x, Wq, Aq, Bq, Wk, Ak, Bk, Wv, Av, Bv, Wp):
        import jax, jax.numpy as jnp
        import numpy as np
        import math
        H = 16
        LORA_SCALING = 16 / 8
        NEG_INF = -1e+30

        def _alibi_slopes(n_heads):
            start = 2.0 ** (-2.0 ** (-(math.log2(n_heads) - 3)))
            return jnp.asarray([start * start ** i for i in range(n_heads)], dtype=jnp.float32)

        def _lora(x, W, A, Bm):
            return x @ W.T + x @ Bm.T @ A.T * LORA_SCALING
        B, T, E = x.shape
        dh = E // H
        q = _lora(x, Wq, Aq, Bq).reshape(B, T, H, dh).transpose(0, 2, 1, 3)
        k = _lora(x, Wk, Ak, Bk).reshape(B, T, H, dh).transpose(0, 2, 1, 3)
        v = _lora(x, Wv, Av, Bv).reshape(B, T, H, dh).transpose(0, 2, 1, 3)
        s = jnp.einsum('bhqd,bhkd->bhqk', q, k) / jnp.sqrt(jnp.float32(dh))
        i = jnp.arange(T)[:, None]
        j = jnp.arange(T)[None, :]
        slopes = _alibi_slopes(H)
        bias = slopes[:, None, None] * (i - j).astype(jnp.float32)
        s = s + bias[None]
        s = jnp.where(j[None, None] <= i[None, None], s, NEG_INF)
        out = jnp.einsum('bhqk,bhkd->bhqd', jax.nn.softmax(s, axis=-1), v)
        out = out.transpose(0, 2, 1, 3).reshape(B, T, E)
        return out @ Wp.T

    def _L0_xattn_ref(x, context, mask, ln1_s, ln1_b, lnc_s, lnc_b, Wq, Wkv, null_kv, Wo, lno_s, lno_b):
        import jax, jax.numpy as jnp
        import numpy as np
        EPS = 1e-06
        NUM_HEADS = 16
        DIM_HEADS = 64

        def _ln(x, scale, bias):
            mu = jnp.mean(x, axis=-1, keepdims=True)
            var = jnp.mean(jnp.square(x - mu), axis=-1, keepdims=True)
            return (x - mu) * jax.lax.rsqrt(var + EPS) * scale + bias
        b, n, _ = x.shape
        h, d = (NUM_HEADS, DIM_HEADS)
        scale = h ** (-0.5)
        xn = _ln(x, ln1_s, ln1_b)
        cn = _ln(context, lnc_s, lnc_b)
        q = xn @ Wq
        kv = cn @ Wkv
        k, v = jnp.split(kv, 2, axis=-1)

        def to_heads(t):
            return t.reshape(t.shape[0], t.shape[1], h, d).transpose(0, 2, 1, 3)
        q, k, v = (to_heads(q), to_heads(k), to_heads(v))
        nk = jnp.broadcast_to(null_kv[0], (b, h, 1, d))
        nv = jnp.broadcast_to(null_kv[1], (b, h, 1, d))
        k = jnp.concatenate((nk, k), axis=2)
        v = jnp.concatenate((nv, v), axis=2)
        sim = jnp.einsum('bhid,bhjd->bhij', q * scale, k)
        mfull = jnp.pad(mask, ((0, 0), (1, 0)), constant_values=True)[:, None, None, :]
        max_neg = -jnp.finfo(sim.dtype).max
        sim = jnp.where(mfull, sim, max_neg)
        attn = jax.nn.softmax(sim, axis=-1)
        out = jnp.einsum('bhij,bhjd->bhid', attn, v)
        out = out.transpose(0, 2, 1, 3).reshape(b, n, h * d)
        out = out @ Wo
        return _ln(out, lno_s, lno_b)

    def _L0_ffn_ref(x, gate_w, balance_bias, w1, w2):
        import jax, jax.numpy as jnp
        import numpy as np
        DIM = 128
        NUM_EXPERTS = 8
        ACTIVE_EXPERTS = 2
        EXPERT_DIM = 256
        B, S, D = x.shape
        T = B * S
        xf = x.reshape(T, D)
        gate_logits = jnp.einsum('td,ed->te', xf, gate_w)
        gate_scores = jax.nn.sigmoid(gate_logits + balance_bias)
        topk_scores, topk_idx = jax.lax.top_k(gate_scores, ACTIVE_EXPERTS)
        topk_scores = topk_scores / (topk_scores.sum(axis=-1, keepdims=True) + 1e-06)
        comb = jnp.zeros((T, NUM_EXPERTS), dtype=x.dtype)
        comb = comb.at[jnp.arange(T)[:, None], topk_idx].add(topk_scores)
        h = jax.nn.silu(jnp.einsum('td,ehd->teh', xf, w1))
        expert_out = jnp.einsum('teh,edh->ted', h, w2)
        out = jnp.einsum('te,ted->td', comb, expert_out)
        return out.reshape(B, S, D)

    def _L1_attn_ref(x, Wq, bq, Wk, bk, Wv, bv, Wo, bo):
        import jax, jax.numpy as jnp
        import numpy as np
        import math
        WINDOW = 64
        N_HEAD = 16
        B, L, D = x.shape
        W, H = (WINDOW, N_HEAD)
        dh = D // H
        C = L // W
        scale = 1.0 / math.sqrt(dh)
        q = x @ Wq.T + bq
        k = x @ Wk.T + bk
        v = x @ Wv.T + bv
        kp = jnp.pad(k, ((0, 0), (W, 0), (0, 0)))
        vp = jnp.pad(v, ((0, 0), (W, 0), (0, 0)))
        idx = jnp.arange(C)[:, None] * W + jnp.arange(2 * W)[None, :]
        kc = kp[:, idx].reshape(B, C, 2 * W, H, dh)
        vc = vp[:, idx].reshape(B, C, 2 * W, H, dh)
        qc = q.reshape(B, C, W, H, dh)
        scores = jnp.einsum('bcqhd,bckhd->bchqk', qc, kc) * scale
        valid = idx >= W
        scores = jnp.where(valid[None, :, None, None, :], scores, jnp.float32(-1000000000.0))
        attn = jax.nn.softmax(scores, axis=-1)
        out = jnp.einsum('bchqk,bckhd->bcqhd', attn, vc).reshape(B, L, D)
        return out @ Wo.T + bo

    def _L1_xattn_ref(q_input, k_input, v_input, key_padding_mask, Wq, bq, Wk, bk, Wv, bv, Wo, bo):
        import jax, jax.numpy as jnp
        import numpy as np
        D_MODEL = 128
        N_HEADS = 16
        HEAD_DIM = D_MODEL // N_HEADS
        B, S = (4, 256)
        b, sq, d = q_input.shape
        sk = k_input.shape[1]
        Q = q_input @ Wq + bq
        K = k_input @ Wk + bk
        V = v_input @ Wv + bv
        Qh = Q.reshape(b, sq, N_HEADS, HEAD_DIM).transpose(0, 2, 1, 3)
        Kh = K.reshape(b, sk, N_HEADS, HEAD_DIM).transpose(0, 2, 1, 3)
        Vh = V.reshape(b, sk, N_HEADS, HEAD_DIM).transpose(0, 2, 1, 3)
        scores = jnp.einsum('bhqd,bhkd->bhqk', Qh, Kh) / jnp.sqrt(jnp.float32(HEAD_DIM))
        causal = jnp.triu(jnp.ones((sq, sk), bool), k=1)[None, None]
        scores = jnp.where(causal, -jnp.inf, scores)
        scores = jnp.where(key_padding_mask[:, None, None, :], -jnp.inf, scores)
        all_inf = jnp.all(jnp.isinf(scores))
        probs = jax.nn.softmax(scores, axis=-1)
        probs = jnp.where(all_inf, jnp.float32(1.0) / sk, probs)
        out = jnp.einsum('bhqk,bhkd->bhqd', probs, Vh)
        out = out.transpose(0, 2, 1, 3).reshape(b, sq, d)
        return out @ Wo + bo

    def _L1_ffn_ref(x, gate_w, gate_b, w1, w2, w3, ws1, ws2, ws3):
        import jax, jax.numpy as jnp
        import numpy as np
        E = 64
        K = 6
        CAP = 64
        ROUTE_SCALE = 1.0
        shape = x.shape
        D = shape[-1]
        xf = x.reshape(-1, D)
        T = xf.shape[0]
        scores = jax.nn.softmax(xf @ gate_w.T, axis=-1)
        _, idx = jax.lax.top_k(scores + gate_b, K)
        weights = jnp.take_along_axis(scores, idx, axis=1) * ROUTE_SCALE
        flat_e = idx.reshape(-1)
        order = jnp.argsort(flat_e)
        se = flat_e[order]
        counts = jnp.bincount(flat_e, length=E)
        starts = jnp.cumsum(counts) - counts
        pos = jnp.arange(T * K) - starts[se]
        tok = order // K
        xb = jnp.zeros((E, CAP, D), xf.dtype).at[se, pos].set(xf[tok], mode='drop')
        h = jax.nn.silu(jnp.einsum('ecd,eid->eci', xb, w1)) * jnp.einsum('ecd,eid->eci', xb, w3)
        yb = jnp.einsum('eci,edi->ecd', h, w2)
        valid = (pos < CAP).astype(xf.dtype)
        contrib = yb[se, jnp.minimum(pos, CAP - 1)]
        wf = weights.reshape(-1)[order] * valid
        y = jnp.zeros_like(xf).at[tok].add(contrib * wf[:, None])
        z = jax.nn.silu(xf @ ws1.T) * (xf @ ws3.T) @ ws2.T
        return (y + z).reshape(shape)
    x = _layernorm(x + _L0_attn_ref(x, L0_attn_Wq, L0_attn_Aq, L0_attn_Bq, L0_attn_Wk, L0_attn_Ak, L0_attn_Bk, L0_attn_Wv, L0_attn_Av, L0_attn_Bv, L0_attn_Wp), axis=-1)
    x = _layernorm(x + _L0_xattn_ref(x, ctx_1024, mask_BxS2_bf1, L0_xattn_ln1_s, L0_xattn_ln1_b, L0_xattn_lnc_s, L0_xattn_lnc_b, L0_xattn_Wq, L0_xattn_Wkv, L0_xattn_null_kv, L0_xattn_Wo, L0_xattn_lno_s, L0_xattn_lno_b), axis=-1)
    x = _layernorm(x + _L0_ffn_ref(x, L0_ffn_gate_w, L0_ffn_balance_bias, L0_ffn_w1, L0_ffn_w2), axis=-1)
    x = _layernorm(x + _L1_attn_ref(x, L1_attn_Wq, L1_attn_bq, L1_attn_Wk, L1_attn_bk, L1_attn_Wv, L1_attn_bv, L1_attn_Wo, L1_attn_bo), axis=-1)
    x = _layernorm(x + _L1_xattn_ref(x, ctx_1024, ctx_1024, mask_BxS2_bk0, L1_xattn_Wq, L1_xattn_bq, L1_xattn_Wk, L1_xattn_bk, L1_xattn_Wv, L1_xattn_bv, L1_xattn_Wo, L1_xattn_bo), axis=-1)
    x = _layernorm(x + _L1_ffn_ref(x, L1_ffn_gate_w, L1_ffn_gate_b, L1_ffn_w1, L1_ffn_w2, L1_ffn_w3, L1_ffn_ws1, L1_ffn_ws2, L1_ffn_ws3), axis=-1)
    return x

_drawn_inputs = setup_inputs


def setup_inputs(seed=0):
    import zlib

    import numpy as np

    out = dict(_drawn_inputs(seed))
    spreads = {'L0_xattn_ln1_s': (1.0, 0.2),
     'L0_xattn_ln1_b': (0.0, 0.1),
     'L0_xattn_lnc_s': (1.0, 0.2),
     'L0_xattn_lnc_b': (0.0, 0.1),
     'L0_xattn_lno_s': (1.0, 0.2),
     'L0_xattn_lno_b': (0.0, 0.1),
     'L0_ffn_balance_bias': (0.0, 0.428),
     'L1_attn_bq': (0.0, 2.0),
     'L1_attn_bk': (0.0, 2.0),
     'L1_attn_bv': (0.0, 0.345),
     'L1_attn_bo': (0.0, 0.1),
     'L1_xattn_bq': (0.0, 0.8),
     'L1_xattn_bk': (0.0, 2.0),
     'L1_xattn_bv': (0.0, 0.383),
     'L1_xattn_bo': (0.0, 0.1),
     'L1_ffn_gate_b': (0.0, 0.8)}
    factors = {'L0_attn_Aq': 8.0,
     'L0_attn_Bq': 8.0,
     'L0_attn_Ak': 8.0,
     'L0_attn_Bk': 8.0,
     'L0_attn_Av': 8.0,
     'L0_attn_Bv': 8.0,
     'L1_attn_Wq': 8.0,
     'L1_attn_Wk': 8.0,
     'L1_xattn_Wq': 8.0,
     'L1_xattn_Wk': 8.0,
     'L1_ffn_gate_w': 8.0,
     'L1_ffn_w1': 8.0,
     'L1_ffn_w2': 8.0,
     'L1_ffn_w3': 8.0,
     'L1_ffn_ws1': 8.0,
     'L1_ffn_ws2': 8.0,
     'L1_ffn_ws3': 8.0,
     'L0_ffn_gate_w': 3.141}
    for name, (base, spread) in spreads.items():
        noise = np.random.default_rng([zlib.crc32(name.encode()), seed]).standard_normal(out[name].shape)
        drawn = base * np.exp(spread * noise) if base else spread * noise
        out[name] = jnp.asarray(drawn.astype(out[name].dtype))
    for name, factor in factors.items():
        out[name] = (out[name] * factor).astype(out[name].dtype)
    return out
```

```python
from contextlib import ExitStack

import numpy as np

import concourse.bass as bass
from concourse import mybir

P = 128
B, T, S2 = 2, 256, 512
N = B * T
NT = N // P
H = 16
DH = P // H
XC = 8
XD = 64
E0, F0, K0 = 8, 256, 2
E1, F1, K1, CAP = 64, 88, 6, 64
W = 64
PAD = T + W
EPS_POST, EPS_X = 1e-5, 1e-6
BIG = 1e30
BLK = 384

F32, F16, BF16, U8 = mybir.dt.float32, mybir.dt.float16, mybir.dt.bfloat16, mybir.dt.uint8
ALU = mybir.AluOpType
ACT = mybir.ActivationFunctionType
AX = mybir.AxisListType.X
ds = bass.ds

COLS = ["ln1_s", "ln1_b", "lnc_s", "lnc_b", "a1_bq", "a1_bk", "a1_bv", "x1_bq", "x1_bk", "x1_bv"]
ROWS = ["lno_s", "lno_b", "a1_bo", "x1_bo"]
C_ID, C_HM, C_SL, C_REL, C_WIN, C_NH, C_HALF, C_LT = 0, 128, 144, 160, 544, 1056, 1184, 1186
C_ALL = C_LT + E0 * E0
G_CUM, G_ONE, G_SLOT = 0, 128, 640
G_ALL = 640 + E1 * CAP


def shape_constants():
    p = np.arange(P)
    c = np.zeros((P, C_ALL), np.float32)
    c[:, C_ID:C_ID + P] = np.eye(P)
    c[:, C_HM:C_HM + H] = p[:, None] // DH == np.arange(H)
    start = 2.0 ** -0.5
    c[:, C_SL:C_SL + H] = -np.float32(start * start ** np.arange(H))
    j = np.arange(P)
    near = np.where(j[None] <= p[:, None], p[:, None] - j[None], -1e34)
    c[:, C_REL:C_REL + BLK] = np.concatenate([near, p[:, None] - j[None] + P, near], 1)
    win = np.zeros((P, 4, P), np.float32)
    win[:W, 0::2, :W] = 1e9
    c[:, C_WIN:C_WIN + 512] = win.reshape(P, 512)
    heads = np.zeros((P, XC, H), np.float32)
    for k in range(XC):
        heads[:XD, k, 2 * k] = 1
        heads[XD:, k, 2 * k + 1] = 1
    c[:, C_NH:C_NH + P] = heads.reshape(P, P)
    c[:, C_HALF:C_HALF + 2] = p[:, None] // XD == np.arange(2)
    c[:, C_LT:C_ALL] = (np.arange(E0)[None] < np.arange(E0)[:, None]).reshape(1, E0 * E0)
    g = np.zeros((P, G_ALL), np.float16)
    g[:, G_CUM:G_CUM + P] = p[:, None] <= j[None]
    g[:, G_ONE:G_ONE + 512] = 1
    g[:, G_SLOT:G_SLOT + E1 * CAP] = np.arange(E1 * CAP)[None] // E1 + 1
    return c, g


def decoder(nc, x, ctx, mask_x0, mask_x1, consts, halfs, cols, rows, gate_rows, lora, w_a0, w_x0, wo_x0, null_kv,
            gate0, w_e0, w_a1, w_x1, gate1, w13_e1, w2_e1, ws13, ws2, out):
    with ExitStack() as stack:
        def sb(name, shape, dt=F32):
            return stack.enter_context(nc.sbuf_tensor(name, shape, dt))

        def sem(name):
            return stack.enter_context(nc.semaphore(name))

        ps = stack.enter_context(nc.psum_tensor("ps", [P, 8, 512], F32))
        PT_BANK, O_BANK, Y_BANK = 4, 6, 7

        cs = sb("cs", [P, C_ALL])
        hs = sb("hs", [P, G_ALL], F16)
        vec = sb("vec", [P, len(COLS)])
        row = sb("row", [P, len(ROWS), P])
        grow = sb("grow", [P, E0 + E1])
        ident = cs[:, C_ID:C_ID + P]
        lora_sb = sb("lora_sb", [8, 6, P])
        wa0 = sb("wa0", [P, 4, P])
        wa1 = sb("wa1", [P, 4, P])
        wx1 = sb("wx1", [P, 4, P])
        x0ring = sb("x0ring", [P, 2, 3, P])
        nkv = sb("nkv", [P, 2])
        wo_all = sb("wo_all", [P, XC, P])
        g0w = sb("g0w", [P, E0])
        g1w = sb("g1w", [P, E1])
        e0w = sb("e0w", [P, E0, 2, F0])
        ws13_sb = sb("ws13_sb", [P, 4, F1])
        ws2_sb = sb("ws2_sb", [F1, 2, P])
        RING = 4
        w13r = sb("w13r", [P, RING, 4, F1])
        w2r = sb("w2r", [F1, RING, 2, P])
        mask_words = sb("mask_words", [P, 2, B, S2 // 4], mybir.dt.uint32)
        maskb = mask_words[:].bitcast(U8)

        X = sb("X", [P, NT, P])
        XB = sb("XB", [P, NT, P])
        R = sb("R", [P, NT, P])
        XT = sb("XT", [P, N])
        XN = sb("XN", [P, NT, P])
        XTP = sb("XTP", [P, B, PAD])
        C = sb("C", [P, 8, P])
        CN = sb("CN", [P, 8, P])
        CNT = sb("CNT", [P, B * S2])
        CT = sb("CT", [P, N])
        QT = sb("QT", [P, N])
        KT = sb("KT", [P, B * PAD])
        V = sb("V", [P, 8, P])
        OT = sb("OT", [P, N])
        Kh = sb("Kh", [P, 2, B * PAD])
        VM = P + 16
        Vh = sb("Vh", [P, 2, 8, VM])
        region = sb("region", [P, 8192])

        def part_of(buffer, first, **sizes):
            names = " ".join(sizes)
            width = int(np.prod(list(sizes.values())))
            return buffer[:, first:first + width].rearrange(f"p ({names}) -> p {names}", **sizes)

        NS = part_of(region, 0, i=2, c=1024)
        PR = part_of(region, 2048, i=2, c=1024)
        PTS = part_of(region, 4096, i=2, c=1024)
        NM = sb("NM", [P, 2, 4])
        MN = sb("MN", [P, 2, 4])
        RS = sb("RS", [P, 2, 4])
        RI = sb("RI", [P, 2, 4])
        zero = sb("zero", [P, 512])
        mhalf = sb("mhalf", [P, 4])
        zcol = sb("zcol", [P, 1])
        st = sb("st", [P, 4, 6])
        mv = sb("mv", [P, 4, 2])
        ve = sb("ve", [P, 4])
        rstd = sb("rstd", [P, 4])
        negpad = sb("negpad", [P, B, S2])
        negrel = sb("negrel", [P, B, BLK])

        zh = sb("zh", [P, P], F16)
        region2 = sb("region2", [P, 5120])
        QC = part_of(region2, 0, i=2, c=N)
        KC = part_of(region2, 1024, i=2, c=B * S2)
        VC = part_of(region2, 3072, i=2, t=8, c=P)
        OC = sb("OC", [P, 2, N])
        nk2 = sb("nk2", [P, 2])
        nv16 = sb("nv16", [P, XC, H])
        nvo = sb("nvo", [H, P])
        SN = sb("SN", [P, 2, NT, 2])
        DN = sb("DN", [P, 2, 2])
        PN = sb("PN", [P, 2, 2])
        TS = sb("TS", [P, 2, 2])
        PNN = sb("PNN", [P, NT, H])
        PNT = sb("PNT", [H, N])
        Z0 = sb("Z0", [P, NT, E0])
        EZ0 = sb("EZ0", [P, NT, E0])
        GS0 = sb("GS0", [P, NT, E0])
        GT0 = sb("GT0", [P, NT, E0, E0])
        EQ0 = sb("EQ0", [P, NT, E0, E0])
        RK0 = sb("RK0", [P, NT, E0])
        SG0 = sb("SG0", [P, NT, E0])
        SM0 = sb("SM0", [P, NT])
        IV0 = sb("IV0", [P, NT])
        comb0 = sb("comb0", [P, NT, E0])
        H0 = part_of(region, 6144, i=2, k=2, c=N)
        all_out = sb("all_out", [P, 1])
        peak_limit = sb("peak_limit", [P, 1])
        MC = sb("MC", [P, B])
        MVB = sb("MVB", [P, B])
        scaled_bq = sb("scaled_bq", [P, 2])
        mean_col = sb("mean_col", [P, 1])
        CNf = CN[:].rearrange("p t d -> p (t d)")
        npf = negpad[:].rearrange("p b s -> p (b s)")
        MX = sb("MX", [P, NT])
        NMX = sb("NMX", [P, NT])
        SX = sb("SX", [P, NT])
        EX = part_of(CNf, 0, t=NT, e=E1)
        SC = part_of(CNf, 256, t=NT, e=E1)
        SB = part_of(CNf, 512, t=NT, e=E1)
        T8 = sb("T8", [P, NT, 8])
        GTM = part_of(CNf, 768, t=NT, e=E1)
        EQM = part_of(npf, 0, t=NT, e=E1)
        LEAD = E1 // 2
        SCAN = sb("SCAN", [P, 2, NT, LEAD + E1])
        ROOM = sb("ROOM", [P, NT])
        SEL = part_of(npf, 256, t=NT, e=E1)
        SELh = sb("SELh", [P, NT, E1], F16)
        WT = part_of(npf, 512, t=NT, e=E1)
        XH = sb("XH", [P, NT, P], F16)
        XL = sb("XL", [P, NT, P], F16)
        QS = sb("QS", [P, NT, E1], F16)
        PH = region[:].bitcast(F16).rearrange("p (t s e) -> p t s e", t=NT, s=CAP)
        XBT = part_of(region2, 0, e=E1, s=CAP)
        e0f = e0w[:].rearrange("p e k f -> p (e k f)")
        ZG = part_of(e0f[0:F1, :], 0, k=2, n=N)
        ZH = part_of(e0f[0:F1, :], 1024, k=2, n=N)
        PM = part_of(e0f, 2048, i=2, n=N)
        GG = sb("GG", [F1, 2, 2 * CAP])
        HG = sb("HG", [F1, 2, 2 * CAP])
        PW = sb("PW", [P, 2, NT, 2 * CAP])
        YS = sb("YS", [P, 2, P])

        class ld:
            x = sem("load_x")
            consts = sem("load_consts")
            halfs = sem("load_halfs")
            lora = sem("load_lora")
            w_a0 = sem("load_w_a0")
            nkv = sem("load_nkv")
            ctx = sem("load_ctx")
            vectors = sem("load_vectors")
            mask = sem("load_mask")
            wo_all = sem("load_wo_all")
            gate0 = sem("load_gate0")
            w_e0 = sem("load_w_e0")
            w_a1 = sem("load_w_a1")
            late = sem("load_late")
        const_ready = sem("const_ready")
        ln_chain = sem("ln_chain")
        ln_var = sem("ln_var")
        ln_rstd = sem("ln_rstd")
        ln_done = sem("ln_done")
        turned = sem("turned")
        turned_out = sem("turned_out")
        weff_ps, weff = sem("weff_ps"), sem("weff")

        class HeadSignals:
            def __init__(self, tag, kind):
                self.kind = kind
                self.proj = sem(tag + "_proj")
                self.act_out = sem(tag + "_act_out")
                self.k_out = sem(tag + "_k_out")
                self.kh_ready = sem(tag + "_kh_ready")
                self.vh_ready = sem(tag + "_vh_ready")
                self.pool_chain = sem(tag + "_pool_chain")
                self.scores = sem(tag + "_scores")
                self.neg = sem(tag + "_neg")
                self.peak = sem(tag + "_peak")
                self.exps = sem(tag + "_exps")
                self.norm_chain = sem(tag + "_norm_chain")
                self.probs = sem(tag + "_probs")
                self.flipped = sem(tag + "_flipped")
                self.flip_act = sem(tag + "_flip_act")
                self.heads = sem(tag + "_heads")
                self.resid = sem(tag + "_resid")
                if kind != "window":
                    self.flip_dve = sem(tag + "_flip_dve")
                if kind == "padded":
                    self.neg_chain = sem(tag + "_neg_chain")
                if kind != "causal":
                    self.bias_added = sem(tag + "_bias_added")

        a0 = HeadSignals("a0", "causal")
        a1 = HeadSignals("a1", "window")
        x1 = HeadSignals("x1", "padded")
        stored = sem("stored")

        class x0:
            q_ps = sem("x0_q_ps")
            k_ps = sem("x0_k_ps")
            v_ps = sem("x0_v_ps")
            sn_ps = sem("x0_sn_ps")
            q = sem("x0_q")
            k = sem("x0_k")
            v = sem("x0_v")
            sn = sem("x0_sn")
            oc = sem("x0_oc")
            scores = sem("x0_scores")
            neg = sem("x0_neg")
            low = sem("x0_low")
            peak = sem("x0_peak")
            exps = sem("x0_exps")
            sums = sem("x0_sums")
            probs = sem("x0_probs")
            flipped = sem("x0_flipped")
            flip_act = sem("x0_flip_act")
            flip_dve = sem("x0_flip_dve")
            heads = sem("x0_heads")
            w_even = sem("x0_w_even")
            w_odd = sem("x0_w_odd")
            null_w = sem("x0_null_w")
            nvo_ps = sem("x0_nvo_ps")
            nvo = sem("x0_nvo")
            pnt_ps = sem("x0_pnt_ps")
            pnt = sem("x0_pnt")
            out = sem("x0_out")
            affine = sem("x0_affine")
            base = sem("x0_base")
            negpad = sem("x0_negpad")
        class e0:
            logits = sem("e0_logits")
            route = sem("e0_route")
            ez = sem("e0_ez")
            comb = sem("e0_comb")
            hidden = sem("e0_hidden")
            silu = sem("e0_silu")
            y = sem("e0_y")
            acc = sem("e0_acc")

        SEL_DONE = 19
        LAST = 3

        def run_steps(eng, steps, step, before=4, unroll=2):
            for t in range(before):
                step(t, t % 2)
            with eng.Fori(before // unroll, steps // unroll) as i:
                for k in range(unroll):
                    step(unroll * i + k, k % 2)
            for t in range(steps, steps + LAST):
                step(t, t % 2)

        def run_pairs(eng, pair):
            for t in range(RING):
                pair(t, t)
            with eng.Fori(1, PAIRS // RING) as i:
                for r in range(RING):
                    pair(RING * i + r, r)
            for t in range(PAIRS, PAIRS + 2):
                pair(t, t % RING)

        def known(t):
            return isinstance(t, int)

        class x1m:
            flag = sem("x1m_flag")
            rel = sem("x1m_rel")
            mean_ps = sem("x1m_mean_ps")
            mean = sem("x1m_mean")
            value_ps = sem("x1m_value_ps")
            value = sem("x1m_value")
            patched = sem("x1m_patched")
            bq = sem("x1m_bq")
        pads = sem("pads")
        class e1:
            logits = sem("e1_logits")
            router = sem("e1_router")
            low = sem("e1_low")
            ex = sem("e1_ex")
            sel = sem("e1_sel")
            count_ps = sem("e1_count_ps")
            queue = sem("e1_queue")
            parts = sem("e1_parts")
            onehot = sem("e1_onehot")
            gather_ps = sem("e1_gather_ps")
            gather_act = sem("e1_gather_act")
            gather_dve = sem("e1_gather_dve")
            zh_ps = sem("e1_zh_ps")
            z_silu = sem("e1_z_silu")
            z_mult = sem("e1_z_mult")
            pw = sem("e1_pw")
            pw_t = sem("e1_pw_t")
            pm = sem("e1_pm")
            hidden = sem("e1_hidden")
            silu = sem("e1_silu")
            hg = sem("e1_hg")
            y = sem("e1_y")
            ys = sem("e1_ys")
            added = sem("e1_added")
            w0 = sem("e1_w0")
            w1 = sem("e1_w1")
            w2 = sem("e1_w2")
            w3 = sem("e1_w3")
        PAIRS = E1 // 2

        block = stack.enter_context(nc.Block())

        @block.sync
        def _(sp):
            sp.dma_start(X[:], x.rearrange("(t p) d -> p t d", p=P)).then_inc(ld.x, 16)
            sp.dma_start(cs[:], consts).then_inc(ld.consts, 16)
            sp.dma_start(lora_sb[:], lora).then_inc(ld.lora, 16)
            sp.dma_start(wa0[:], w_a0).then_inc(ld.w_a0, 16)
            sp.dma_start(C[:], ctx.rearrange("(t p) d -> p t d", p=P)).then_inc(ld.ctx, 16)
            sp.dma_start(vec[:], cols).then_inc(ld.vectors, 16)
            sp.dma_start(row[:], rows.broadcast_to([P, len(ROWS), P])).then_inc(ld.vectors, 16)
            sp.dma_start(grow[:], gate_rows.broadcast_to([P, E0 + E1])).then_inc(ld.vectors, 16)
            sp.dma_start(mask_words[:, 0], mask_x0.broadcast_to([P, B, S2 // 4])).then_inc(ld.mask, 16)
            sp.dma_start(mask_words[:, 1], mask_x1.broadcast_to([P, B, S2 // 4])).then_inc(ld.mask, 16)
            sp.dma_start(hs[:], halfs).then_inc(ld.halfs, 16)
            sp.dma_start(wo_all[:], wo_x0).then_inc(ld.wo_all, 16)
            sp.dma_start(g0w[:], gate0).then_inc(ld.gate0, 16)
            sp.dma_start(e0w[:], w_e0).then_inc(ld.w_e0, 16)
            sp.dma_start(wa1[:], w_a1).then_inc(ld.w_a1, 16)
            sp.dma_start(wx1[:], w_x1).then_inc(ld.late, 16)
            sp.dma_start(g1w[:], gate1).then_inc(ld.late, 16)
            sp.dma_start(ws13_sb[:], ws13).then_inc(ld.late, 16)
            sp.dma_start(ws2_sb[:], ws2).then_inc(ld.late, 16)
            sp.dma_start(nkv[:], null_kv).then_inc(ld.nkv, 16)
            sp.dma_start(x0ring[:, 0], w_x0[0]).then_inc(x0.w_even, 16)
            sp.dma_start(x0ring[:, 1], w_x0[1]).then_inc(x0.w_odd, 16)
            with sp.Fori(1, XC // 2) as i:
                for k, arrived in ((0, x0.w_even), (1, x0.w_odd)):
                    sp.wait_ge(x0.v_ps, 2 * i + k - 1)
                    sp.dma_start(x0ring[:, k], w_x0[ds(2 * i + k, 1)].rearrange("a p k d -> (a p) k d")).then_inc(arrived, 16)
            ring_full = (e1.w0, e1.w1, e1.w2, e1.w3)
            for r in range(RING):
                sp.dma_start(w13r[:, r], w13_e1[r]).then_inc(ring_full[r], 16)
                sp.dma_start(w2r[:, r], w2_e1[r]).then_inc(ring_full[r], 16)
            with sp.Fori(1, PAIRS // RING) as i:
                for r in range(RING):
                    sp.wait_ge(e1.y, RING * i + r - RING + 1)
                    sp.dma_start(w13r[:, r], w13_e1[ds(RING * i + r, 1)].rearrange("a p k d -> (a p) k d")
                                 ).then_inc(ring_full[r], 16)
                    sp.dma_start(w2r[:, r], w2_e1[ds(RING * i + r, 1)].rearrange("a p k d -> (a p) k d")
                                 ).then_inc(ring_full[r], 16)
            sp.wait_ge(ln_done, 10)
            sp.dma_start(out.rearrange("(t p) d -> p t d", p=P), X[:]).then_inc(stored, 16)
            sp.wait_ge(stored, 16)

        @block.gpsimd
        def _(pool):
            nc.gpsimd.memset(zero[:], 0.0)
            nc.gpsimd.memset(mhalf[:], -0.5)
            nc.gpsimd.memset(zcol[:], 0.0)
            nc.gpsimd.memset(zh[:], 0.0)
            nc.gpsimd.memset(mean_col[:], 1.0 / S2)
            nc.gpsimd.memset(SCAN[:], 0.0)
            nc.gpsimd.memset(Vh[:], 0.0)
            nc.gpsimd.memset(XTP[:], 0.0).then_inc(const_ready, 1)
            pool.wait_ge(ld.consts, 16)

            def root(n):
                pool.wait_ge(const_ready, 1)
                pool.wait_ge(ln_var, n + 1)
                nc.gpsimd.tensor_tensor(rstd[:], ve[:], mhalf[:], ALU.pow).then_inc(ln_rstd, 1)

            def masked_heads(s):
                window = s.kind == "window"
                width = B * PAD if window else N
                tiles = 8 if window else NT
                pool.wait_ge(s.k_out, 1)
                pool.wait_ge(s.act_out, 2)
                pool.wait_ge(const_ready, 1)

                def step(t, p):
                    if not known(t) or t < H:
                        if not known(t) or t >= 2:
                            pool.wait_ge(s.scores, t - 1)
                            pool.wait_ge(const_ready, 1)
                        nc.gpsimd.tensor_tensor(Kh[:, p, 0:width], KT[:, 0:width],
                                                cs[:, ds(t + C_HM, 1)].broadcast_to([P, width]),
                                                ALU.mult).then_inc(s.kh_ready, 1)
                    if not known(t) or t >= 2:
                        if not known(t) or t >= 4:
                            pool.wait_ge(s.heads, t - 3)
                            pool.wait_ge(const_ready, 1)
                        nc.gpsimd.tensor_copy(Vh[:, p, 0:tiles, ds(8 * t - 16, 8)],
                                              zero[:, 0:8 * tiles].rearrange("p (t d) -> p t d", t=tiles)
                                              ).then_inc(s.pool_chain, 1)
                        pool.wait_ge(s.pool_chain, t - 1)
                        pool.wait_ge(const_ready, 1)
                        nc.gpsimd.tensor_copy(Vh[:, p, 0:tiles, ds(8 * t, 8)],
                                              V[:, 0:tiles, ds(8 * t - 16, 8)]).then_inc(s.vh_ready, 1)

                for t in range(4):
                    step(t, t % 2)
                with pool.Fori(2, H // 2) as i:
                    step(2 * i, 0)
                    step(2 * i + 1, 1)
                step(H, 0)
                step(H + 1, 1)
                for p in range(2):
                    pool.wait_ge(s.heads, H)
                    nc.gpsimd.tensor_copy(Vh[:, p, 0:tiles, 8 * (H + p):8 * (H + p) + 8],
                                          zero[:, 0:8 * tiles].rearrange("p (t d) -> p t d", t=tiles)
                                          ).then_inc(s.pool_chain, 1)
                pool.wait_ge(s.pool_chain, H + 2)

            root(0)
            root(1)
            masked_heads(a0)
            root(2)
            pool.wait_ge(ln_done, 3)
            pool.wait_ge(ld.vectors, 48)
            nc.gpsimd.tensor_tensor(XB[:], X[:], row[:, 1, :].unsqueeze(1).broadcast_to([P, NT, P]),
                                    ALU.add).then_inc(x0.base, 1)
            root(3)
            root(4)
            root(5)
            root(6)
            nc.gpsimd.memset(KT[:].rearrange("p (b k) -> p b k", b=B)[:, :, 0:W], 0.0).then_inc(pads, 1)
            pool.wait_ge(pads, 1)
            pool.wait_ge(ln_done, 7)
            nc.gpsimd.tensor_tensor(XB[:], X[:], row[:, 2, :].unsqueeze(1).broadcast_to([P, NT, P]),
                                    ALU.add).then_inc(a1.bias_added, 1)
            masked_heads(a1)
            root(7)
            pool.wait_ge(ln_done, 8)
            nc.gpsimd.tensor_tensor(XB[:], X[:], row[:, 3, :].unsqueeze(1).broadcast_to([P, NT, P]),
                                    ALU.add).then_inc(x1.bias_added, 1)
            masked_heads(x1)
            root(8)
            root(9)

        @block.tensor
        def _(pe):
            def turn(n, k, bank=Y_BANK):
                for t in range(NT):
                    last = nc.tensor.transpose(ps[:, bank, t * P:(t + 1) * P], k[:, t, :], ident)
                last.then_inc(turned, 1)

            def head_steps(s):
                window = s.kind == "window"
                qw = W if window else P

                def step(t, p):
                    if not known(t) or t < H:
                        pe.wait_ge(s.kh_ready, t + 1)
                        if not known(t) or t >= 2:
                            pe.wait_ge(s.neg, t - 1)
                        for b in range(B):
                            if window:
                                for c in range(T // W):
                                    last = nc.tensor.matmul(
                                        ps[W * (c % 2):W * (c % 2) + W, 2 * p, ds((2 * b + c // 2) * P, P)],
                                        QT[:, b * T + c * W:b * T + (c + 1) * W],
                                        Kh[:, p, b * PAD + c * W:b * PAD + c * W + 2 * W], start=True, stop=True)
                            else:
                                nc.tensor.matmul(ps[:, 2 * p + b, 0:P], QT[:, b * T:b * T + P],
                                                 Kh[:, p, b * T:b * T + P], start=True, stop=True)
                                last = nc.tensor.matmul(ps[:, 2 * p + b, P:3 * P], QT[:, b * T + P:b * T + T],
                                                        Kh[:, p, b * T:b * T + T], start=True, stop=True)
                        last.then_inc(s.scores, 1)
                    if not known(t) or 2 <= t < H + 2:
                        pe.wait_ge(s.probs, t - 1)
                        if not known(t) or t >= 3:
                            pe.wait_ge(s.flip_act, t - 2)
                            if not window:
                                pe.wait_ge(s.flip_dve, t - 2)
                        if window:
                            for k in range(4):
                                last = nc.tensor.transpose(ps[:, PT_BANK, k * P:(k + 1) * P],
                                                           PR[:, p, k * P:(k + 1) * P], ident)
                        else:
                            for b in range(B):
                                for k in range(3):
                                    last = nc.tensor.transpose(ps[:, PT_BANK + b, k * P:(k + 1) * P],
                                                               PR[:, p, b * BLK + k * P:b * BLK + (k + 1) * P], ident)
                        last.then_inc(s.flipped, 1)
                    if not known(t) or t >= 3:
                        q = 1 - p
                        pe.wait_ge(s.flip_act, t - 2)
                        if not window:
                            pe.wait_ge(s.flip_dve, t - 2)
                        pe.wait_ge(s.vh_ready, t - 2)
                        for b in range(B):
                            if window:
                                for c in range(T // W):
                                    last = nc.tensor.matmul(
                                        ps[:, O_BANK, b * T + c * W:b * T + (c + 1) * W],
                                        Vh[:, q, b * 4 + c, 16:16 + P],
                                        PTS[:, q, (2 * b + c // 2) * P + W * (c % 2):(2 * b + c // 2) * P + W * (c % 2) + W],
                                        start=False, stop=False, skip_group_check=True)
                            else:
                                nc.tensor.matmul(ps[:, O_BANK, b * T:b * T + T], Vh[:, q, 2 * b, 16:16 + P],
                                                 PTS[:, q, b * BLK:b * BLK + T],
                                                 start=False, stop=False, skip_group_check=True)
                                last = nc.tensor.matmul(ps[:, O_BANK, b * T + P:b * T + T], Vh[:, q, 2 * b + 1, 16:16 + P],
                                                        PTS[:, q, b * BLK + T:b * BLK + BLK],
                                                        start=False, stop=False, skip_group_check=True)
                        last.then_inc(s.heads, 1)

                nc.tensor.matmul(ps[:, O_BANK, :], zh[:],
                                 hs[:, G_ONE:G_ONE + 512], start=True, stop=False, skip_group_check=True)
                run_steps(pe, H, step)

            def out_proj(s, w):
                pe.wait_ge(s.act_out, 3)
                for t in range(NT):
                    last = nc.tensor.matmul(ps[:, Y_BANK, t * P:(t + 1) * P], OT[:, t * P:(t + 1) * P], w[:, 3, :],
                                            start=True, stop=True)
                last.then_inc(s.proj, 1)

            pe.wait_ge(ld.lora, 16)
            for k in range(3):
                last = nc.tensor.matmul(ps[:, 0, k * P:(k + 1) * P], lora_sb[:, k, :], lora_sb[:, 3 + k, :],
                                        start=True, stop=True)
            last.then_inc(weff_ps, 1)
            pe.wait_ge(ld.x, 16)
            pe.wait_ge(ld.consts, 16)
            turn(0, X)
            pe.wait_ge(weff, 1)
            pe.wait_ge(turned_out, 1)
            nc.tensor.matmul(ps[:, 1, :], wa0[:, 0, :], XT[:], start=True, stop=True).then_inc(a0.proj, 1)
            nc.tensor.matmul(ps[:, 2, :], wa0[:, 1, :], XT[:], start=True, stop=True).then_inc(a0.proj, 1)
            for t in range(NT):
                last = nc.tensor.matmul(ps[:, 3, t * P:(t + 1) * P], XT[:, t * P:(t + 1) * P], wa0[:, 2, :],
                                        start=True, stop=True)
            last.then_inc(a0.proj, 1)
            pe.wait_ge(a0.act_out, 2)
            pe.wait_ge(a0.k_out, 1)
            pe.wait_ge(ld.halfs, 16)
            pe.wait_ge(const_ready, 1)
            head_steps(a0)
            out_proj(a0, wa0)

            for k, src in enumerate((CN[:, 0:4], CN[:, 4:8], None)):
                if src is not None:
                    pe.wait_ge(ln_done, k + 1)
                    turn(k, src, k)
                else:
                    pe.wait_ge(ld.ctx, 16)
                    for t in range(NT):
                        last = nc.tensor.transpose(ps[:, 2, t * P:(t + 1) * P], C[:, 4 * (t // 2) + t % 2, :], ident)
                    last.then_inc(turned, 1)
            pe.wait_ge(x0.null_w, 1)
            pe.wait_ge(ld.wo_all, 16)
            for c in range(XC):
                last = nc.tensor.matmul(ps[0:H, 3, 0:P], nv16[:, c, :], wo_all[:, c, :],
                                        start=(c == 0), stop=(c == XC - 1))
            last.then_inc(x0.nvo_ps, 1)

            def project_q(c, p):
                pe.wait_ge(x0.w_odd if p else x0.w_even, 16 * (c // 2 + 1) if known(c) else (c - p) * 8 + 16)
                nc.tensor.matmul(ps[:, 0, :], x0ring[:, p, 0, :], XT[:], start=True, stop=True).then_inc(x0.q_ps, 1)

            def project_k(c, p):
                for b in range(B):
                    last = nc.tensor.matmul(ps[:, 2 + b, :], x0ring[:, p, 1, :], CNT[:, b * S2:(b + 1) * S2],
                                            start=True, stop=True)
                last.then_inc(x0.k_ps, 1)

            def project_v(c, p):
                for t in range(8):
                    last = nc.tensor.matmul(ps[:, t // 4, (t % 4) * P:(t % 4 + 1) * P], CNT[:, t * P:(t + 1) * P],
                                            x0ring[:, p, 2, :], start=True, stop=True)
                last.then_inc(x0.v_ps, 1)

            def null_scores(c, p):
                pe.wait_ge(x0.q, c + 1)
                for t in range(NT):
                    last = nc.tensor.matmul(ps[:, 2, 2 * t:2 * t + 2], QC[:, p, t * P:(t + 1) * P], nk2[:],
                                            start=True, stop=True)
                last.then_inc(x0.sn_ps, 1)

            def out_chunk(c, p):
                for t in range(NT):
                    nc.tensor.matmul(ps[:, Y_BANK, t * P:(t + 1) * P], OC[:, p, t * P:(t + 1) * P],
                                            wo_all[:, ds(c, 1), :].rearrange("p a d -> p (a d)"),
                                            start=False, stop=False, skip_group_check=True)

            def unit(c, cp, j, last_chunk=False):
                u, p = 4 * c + j, j % 2
                if not known(u) or u < 4 * XC:
                    if j == 0:
                        pe.wait_ge(x0.v, c + 1)
                    elif j == 1:
                        pe.wait_ge(x0.sn, c + 1)
                    elif last_chunk:
                        pe.wait_ge(x0.neg, u - 1)
                    else:
                        pe.wait_ge(x0.k if j == 3 else x0.q, c + 2)
                    b, r = j // 2, XD * p
                    for k in range(2):
                        last = nc.tensor.matmul(ps[:, 2 * p + k, :], QC[r:r + XD, cp, b * T + k * P:b * T + (k + 1) * P],
                                                KC[r:r + XD, cp, b * S2:(b + 1) * S2], start=True, stop=True)
                    last.then_inc(x0.scores, 1)
                if not known(u) or 2 <= u < 4 * XC + 2:
                    pe.wait_ge(x0.probs, u - 1)
                    if not known(u) or u >= 3:
                        pe.wait_ge(x0.flip_act, u - 2)
                        pe.wait_ge(x0.flip_dve, u - 2)
                    for kt in range(4):
                        for k in range(2):
                            last = nc.tensor.transpose(
                                ps[:, PT_BANK + kt // 2, (kt % 2) * T + k * P:(kt % 2) * T + (k + 1) * P],
                                PR[:, p, k * S2 + kt * P:k * S2 + (kt + 1) * P], ident)
                    last.then_inc(x0.flipped, 1)
                if not known(u) or u >= 3:
                    vp, w = (cp, 0) if j == 3 else (1 - cp, j + 1)
                    pe.wait_ge(x0.flip_act, u - 2)
                    pe.wait_ge(x0.flip_dve, u - 2)
                    if j == 3 and (not known(c) or c >= 1):
                        pe.wait_ge(x0.oc, c)
                        out_chunk(c - 1, 1 - cp)
                    b, r = w // 2, XD * (w % 2)
                    if j < 3 or not known(c) or c < XC:
                        for kt in range(4):
                            last = nc.tensor.matmul(ps[r:r + XD, O_BANK, b * T:(b + 1) * T],
                                                    VC[:, vp, 4 * b + kt, r:r + XD],
                                                    PTS[:, 1 - p, kt * T:(kt + 1) * T],
                                                    start=(kt == 0), stop=(kt == 3))
                        last.then_inc(x0.heads, 1)
                if not known(u) or u < 4 * XC:
                    if j == 1 and not last_chunk:
                        pe.wait_ge(x0.neg, 4 * c + 1)
                        project_q(c + 1, 1 - cp)
                        pe.wait_ge(x0.neg, 4 * c + 2)
                        project_k(c + 1, 1 - cp)
                    if j == 3 and not last_chunk:
                        pe.wait_ge(x0.neg, 4 * c + 3)
                        project_v(c + 1, 1 - cp)
                        pe.wait_ge(x0.neg, 4 * c + 4)
                        null_scores(c + 1, 1 - cp)

            pe.wait_ge(ln_done, 4)
            pe.wait_ge(a0.resid, 1)
            turn(3, XN)
            pe.wait_ge(turned_out, 5)
            project_q(0, 0)
            project_k(0, 0)
            pe.wait_ge(x0.q, 1)
            project_v(0, 0)
            pe.wait_ge(x0.k, 1)
            null_scores(0, 0)
            nc.tensor.matmul(ps[:, Y_BANK, :], zh[:], hs[:, G_ONE:G_ONE + 512], start=True, stop=False,
                             skip_group_check=True)
            for j in range(8):
                unit(j // 4, j // 4, j % 4)
            with pe.Fori(1, XC // 2 - 1) as i:
                for j in range(8):
                    unit(2 * i + j // 4, j // 4, j % 4)
            for j in range(8):
                unit(XC - 2 + j // 4, j // 4, j % 4, last_chunk=j >= 4)
            for j in range(3):
                unit(XC, 0, j)
            pe.wait_ge(x0.oc, XC)
            out_chunk(XC - 1, 1)
            pe.wait_ge(x0.probs, 4 * XC)
            for t in range(NT):
                last = nc.tensor.transpose(ps[0:H, 0, t * P:(t + 1) * P], PNN[:, t, :], ident)
            last.then_inc(x0.pnt_ps, 1)
            pe.wait_ge(x0.pnt, 1)
            pe.wait_ge(x0.nvo, 1)
            for t in range(NT):
                last = nc.tensor.matmul(ps[:, Y_BANK, t * P:(t + 1) * P], PNT[:, t * P:(t + 1) * P], nvo[:],
                                        start=False, stop=False, skip_group_check=True)
            last.then_inc(x0.out, 1)

            pe.wait_ge(ln_done, 6)
            turn(5, X, 0)
            pe.wait_ge(turned_out, 6)
            pe.wait_ge(ld.gate0, 16)
            for t in range(NT):
                last = nc.tensor.matmul(ps[:, Y_BANK, t * E0:(t + 1) * E0], XT[:, t * P:(t + 1) * P], g0w[:],
                                        start=True, stop=True)
            last.then_inc(e0.logits, 1)
            pe.wait_ge(ld.w_e0, 16)

            def hidden(e):
                for k in range(2):
                    if e >= 2:
                        pe.wait_ge(e0.silu, 2 * (e - 2) + k + 1)
                    nc.tensor.matmul(ps[:, 2 * (e % 2) + k, :], e0w[:, e, 0, k * P:(k + 1) * P], XT[:],
                                     start=True, stop=True).then_inc(e0.hidden, 1)

            hidden(0)
            for e in range(E0):
                if e + 1 < E0:
                    hidden(e + 1)
                pe.wait_ge(e0.silu, 2 * e + 2)
                if e >= 2:
                    pe.wait_ge(e0.acc, e - 1)
                for t in range(NT):
                    for k in range(2):
                        last = nc.tensor.matmul(ps[:, 4 + e % 2, t * P:(t + 1) * P], H0[:, e % 2, k, t * P:(t + 1) * P],
                                                e0w[:, e, 1, k * P:(k + 1) * P], start=(k == 0), stop=(k == 1))
                last.then_inc(e0.y, 1)

            pe.wait_ge(ln_done, 7)
            turn(6, X)
            pe.wait_ge(turned_out, 7)
            pe.wait_ge(ld.w_a1, 16)
            nc.tensor.matmul(ps[:, 0, :].rearrange("p (b t) -> p b t", b=B), wa1[:, 0, :], XTP[:, :, W:],
                             start=True, stop=True).then_inc(a1.proj, 1)
            nc.tensor.matmul(ps[:, 1, :].rearrange("p (b t) -> p b t", b=B), wa1[:, 1, :], XTP[:, :, W:],
                             start=True, stop=True).then_inc(a1.proj, 1)
            for b in range(B):
                for c in range(T // W):
                    last = nc.tensor.matmul(ps[:, 2 + b, c * P:(c + 1) * P], XTP[:, b, c * W:c * W + 2 * W],
                                            wa1[:, 2, :], start=True, stop=True)
            last.then_inc(a1.proj, 1)
            pe.wait_ge(a1.act_out, 2)
            pe.wait_ge(a1.k_out, 1)
            head_steps(a1)
            out_proj(a1, wa1)

            pe.wait_ge(ld.late, 64)
            nc.tensor.matmul(ps[:, 1, :], wx1[:, 1, :], CT[:], start=True, stop=True).then_inc(x1.proj, 1)
            for t in range(NT):
                last = nc.tensor.matmul(ps[:, 2, t * P:(t + 1) * P], CT[:, t * P:(t + 1) * P], wx1[:, 2, :],
                                        start=True, stop=True)
            last.then_inc(x1.proj, 1)
            for b in range(B):
                for t in range(4):
                    last = nc.tensor.matmul(ps[:, 3, b:b + 1], C[:, 4 * b + t, :], mean_col[:],
                                            start=(t == 0), stop=(t == 3))
            last.then_inc(x1m.mean_ps, 1)
            pe.wait_ge(x1m.mean, 1)
            nc.tensor.matmul(ps[:, 4, 0:B], wx1[:, 2, :], MC[:], start=True, stop=True).then_inc(x1m.value_ps, 1)
            pe.wait_ge(ln_done, 8)
            turn(7, X)
            pe.wait_ge(turned_out, 8)
            nc.tensor.matmul(ps[:, 0, :], wx1[:, 0, :], XT[:], start=True, stop=True).then_inc(x1.proj, 1)
            pe.wait_ge(x1.act_out, 2)
            pe.wait_ge(x1.k_out, 1)
            pe.wait_ge(x1m.value, 1)
            head_steps(x1)
            pe.wait_ge(x1m.patched, 1)
            out_proj(x1, wx1)

            pe.wait_ge(ln_done, 9)
            turn(8, X)
            pe.wait_ge(turned_out, 9)
            pe.wait_ge(ld.late, 64)
            for t in range(NT):
                last = nc.tensor.matmul(ps[:, 4, t * E1:(t + 1) * E1], XT[:, t * P:(t + 1) * P], g1w[:],
                                        start=True, stop=True)
            last.then_inc(e1.logits, 1)
            pe.wait_ge(ld.late, 64)
            for k in range(4):
                last = nc.tensor.matmul(ps[0:F1, k, :], ws13_sb[:, k, :], XT[:], start=True, stop=True)
            last.then_inc(e1.zh_ps, 1)
            pe.wait_ge(e1.z_mult, 1)
            for t in range(NT):
                for k in range(2):
                    nc.tensor.matmul(ps[:, O_BANK, t * P:(t + 1) * P], ZH[:, k, t * P:(t + 1) * P], ws2_sb[:, k, :],
                                     start=(t == 0 and k == 0), stop=False, skip_group_check=True)
            pe.wait_ge(e1.sel, SEL_DONE)
            for t in range(NT):
                for j in range(t + 1):
                    g = G_CUM if j == t else G_ONE
                    last = nc.tensor.matmul(ps[:, 5, t * E1:(t + 1) * E1], hs[:, g:g + P], SELh[:, j, :],
                                            start=(j == 0), stop=(j == t))
            last.then_inc(e1.count_ps, 1)
            pe.wait_ge(e1.parts, 2)
            for g in range(8):
                for t in range(NT):
                    if g == 0 or t == 0:
                        pe.wait_ge(e1.onehot, t + 1 if g == 0 else NT)
                    if t == 0 and g >= 4:
                        pe.wait_ge(e1.gather_dve if g % 2 else e1.gather_act, (g - 4) // 2 + 1)
                    for part in (XH, XL):
                        last = nc.tensor.matmul(ps[:, g % 4, :], part[:, t, :],
                                                PH[:, t, 8 * g:8 * g + 8, :].rearrange("p s e -> p (s e)"),
                                                start=(t == 0 and part is XH), stop=(t == NT - 1 and part is XL))
                last.then_inc(e1.gather_ps, 1)
            pe.wait_ge(e1.gather_act, 4)
            pe.wait_ge(e1.gather_dve, 4)
            ring_full = (e1.w0, e1.w1, e1.w2, e1.w3)

            def pair(t, r):
                p = r % 2
                if not known(t) or t < PAIRS:
                    pe.wait_ge(e1.pw, t + 1)
                    if not known(t) or t >= 2:
                        pe.wait_ge(e1.pm, t - 1)
                    for k in range(NT):
                        last = nc.tensor.transpose(ps[:, p, k * P:(k + 1) * P], PW[:, p, k, :], ident)
                    last.then_inc(e1.pw_t, 1)
                    if not known(t) or t >= 2:
                        pe.wait_ge(e1.hg, t - 1)
                    pe.wait_ge(ring_full[r], ((t - r) * (32 // RING) + 32) if not known(t) else 32 * (t // RING + 1))
                    for k in range(4):
                        last = nc.tensor.matmul(ps[0:F1, 2 + p, k * CAP:(k + 1) * CAP], w13r[:, r, 2 * (k % 2) + k // 2, :],
                                                XBT[:, ds(2 * t + k % 2, 1), :].rearrange("p e s -> p (e s)"),
                                                start=True, stop=True)
                    last.then_inc(e1.hidden, 1)
                if not known(t) or 1 <= t < PAIRS + 1:
                    q, rr = 1 - p, (r - 1) % RING
                    pe.wait_ge(e1.hg, t)
                    if not known(t) or t >= 3:
                        pe.wait_ge(e1.ys, t - 2)
                    for k in range(2):
                        last = nc.tensor.matmul(ps[k * CAP:(k + 1) * CAP, 4 + q, 0:P], HG[:, q, k * CAP:(k + 1) * CAP],
                                                w2r[:, rr, k, :], start=True, stop=True)
                    last.then_inc(e1.y, 1)
                if not known(t) or t >= 2:
                    pe.wait_ge(e1.ys, t - 1)
                    for k in range(NT):
                        last = nc.tensor.matmul(ps[:, O_BANK, k * P:(k + 1) * P], PM[:, p, k * P:(k + 1) * P], YS[:, p, :],
                                                start=False, stop=False, skip_group_check=True)
                    last.then_inc(e1.added, 1)

            run_pairs(pe, pair)

        @block.scalar
        def _(act):
            nc.scalar.preload_act_table(ACT.Exp)

            def head_steps(s):
                window = s.kind == "window"

                def step(t, p):
                    if not known(t) or t < H:
                        act.wait_ge(s.peak, t + 1)
                        if not known(t) or t >= 2:
                            act.wait_ge(s.flipped, t - 1)
                        if window:
                            parts = [(k * P, P, k) for k in range(4)]
                        else:
                            parts = [(b * BLK + a, w, 2 * b + k) for b in range(B)
                                     for k, (a, w) in enumerate(((0, P), (P, 2 * P)))]
                        for a, w, k in parts:
                            last = nc.scalar.activation(PR[:, p, a:a + w], NS[:, p, a:a + w], ACT.Exp,
                                                        bias=NM[:, p, k:k + 1], scale=-1.0,
                                                        accum_out=RS[:, p, k:k + 1])
                        last.then_inc(s.exps, 1)
                    if not known(t) or 2 <= t < H + 2:
                        act.wait_ge(s.flipped, t - 1)
                        if not known(t) or t >= 4:
                            act.wait_ge(s.heads, t - 3)
                        w = 512 if window else BLK
                        nc.scalar.copy(PTS[:, p, 0:w], ps[:, PT_BANK, 0:w]).then_inc(s.flip_act, 1)

                run_steps(act, H, step)

            def heads_out(s, bias):
                act.wait_ge(s.heads, H)
                nc.scalar.activation(OT[:], ps[:, O_BANK, :], ACT.Identity, bias=bias).then_inc(s.act_out, 1)

            act.wait_ge(turned, 1)
            nc.scalar.copy(XT[:], ps[:, Y_BANK, :]).then_inc(turned_out, 1)
            act.wait_ge(a0.proj, 1)
            nc.scalar.mul(QT[:], ps[:, 1, :], DH ** -0.5).then_inc(a0.act_out, 1)
            act.wait_ge(a0.proj, 3)
            nc.scalar.copy(V[:, 0:NT, :], ps[:, 3, :].rearrange("p (t d) -> p t d", t=NT)).then_inc(a0.act_out, 1)
            head_steps(a0)
            act.wait_ge(const_ready, 1)
            heads_out(a0, zcol[:])

            act.wait_ge(ld.vectors, 48)
            for k in range(2):
                act.wait_ge(turned, k + 2)
                nc.scalar.activation(CNT[:, k * S2:(k + 1) * S2], ps[:, k, :], ACT.Identity, bias=vec[:, 3:4],
                                     scale=vec[:, 2:3]).then_inc(turned_out, 1)
            act.wait_ge(turned, 4)
            nc.scalar.copy(CT[:], ps[:, 2, :]).then_inc(turned_out, 1)
            act.wait_ge(x0.nvo_ps, 1)
            nc.scalar.copy(nvo[:], ps[0:H, 3, 0:P]).then_inc(x0.nvo, 1)
            act.wait_ge(turned, 5)
            nc.scalar.activation(XT[:], ps[:, Y_BANK, :], ACT.Identity, bias=vec[:, 1:2],
                                 scale=vec[:, 0:1]).then_inc(turned_out, 1)

            def q_out(c, p):
                act.wait_ge(x0.q_ps, c + 1)
                nc.scalar.mul(QC[:, p, :], ps[:, 0, :], -H ** -0.5).then_inc(x0.q, 1)

            def k_out(c, p):
                act.wait_ge(x0.k_ps, c + 1)
                nc.scalar.copy(KC[:, p, :].rearrange("p (b k) -> p b k", b=B), ps[:, 2:4, :]).then_inc(x0.k, 1)

            def v_out(c, p):
                act.wait_ge(x0.v_ps, c + 1)
                nc.scalar.copy(VC[:, p, :, :].rearrange("p (b t) d -> p b (t d)", b=2), ps[:, 0:2, :]).then_inc(x0.v, 1)

            def unit(c, cp, j, last_chunk=False):
                u, p = 4 * c + j, j % 2
                if not known(u) or u < 4 * XC:
                    act.wait_ge(x0.peak, u + 1)
                    if not known(u) or u >= 2:
                        act.wait_ge(x0.flipped, u - 1)
                    for k in range(2):
                        nc.scalar.activation(PR[:, p, k * S2:(k + 1) * S2], NS[:, p, k * S2:(k + 1) * S2], ACT.Exp,
                                             bias=NM[:, p, k:k + 1], scale=-1.0, accum_out=RS[:, p, k:k + 1])
                    nc.scalar.activation(PN[:, p, :], DN[:, p, :], ACT.Exp).then_inc(x0.exps, 1)
                if not known(u) or 2 <= u < 4 * XC + 2:
                    act.wait_ge(x0.flipped, u - 1)
                    if not known(u) or u >= 4:
                        act.wait_ge(x0.heads, u - 3)
                    nc.scalar.copy(PTS[:, p, 0:512], ps[:, PT_BANK, :]).then_inc(x0.flip_act, 1)
                if (not known(u) or u < 4 * XC) and not last_chunk:
                    if j == 1:
                        q_out(c + 1, 1 - cp)
                        k_out(c + 1, 1 - cp)
                    if j == 3:
                        v_out(c + 1, 1 - cp)
                if j == 2 and (not known(c) or c >= 1):
                    act.wait_ge(x0.heads, 4 * c)
                    nc.scalar.copy(OC[:, 1 - cp, :], ps[:, O_BANK, :]).then_inc(x0.oc, 1)

            q_out(0, 0)
            k_out(0, 0)
            v_out(0, 0)
            for j in range(8):
                unit(j // 4, j // 4, j % 4)
            with act.Fori(1, XC // 2 - 1) as i:
                for j in range(8):
                    unit(2 * i + j // 4, j // 4, j % 4)
            for j in range(8):
                unit(XC - 2 + j // 4, j // 4, j % 4, last_chunk=j >= 4)
            for j in range(3):
                unit(XC, 0, j)
            act.wait_ge(x0.pnt_ps, 1)
            nc.scalar.copy(PNT[:], ps[0:H, 0, :]).then_inc(x0.pnt, 1)

            act.wait_ge(turned, 6)
            nc.scalar.copy(XT[:], ps[:, 0, :]).then_inc(turned_out, 1)
            act.wait_ge(e0.route, 1)
            nc.scalar.activation(EZ0[:], Z0[:], ACT.Exp, scale=-1.0).then_inc(e0.ez, 1)
            for e in range(E0):
                for k in range(2):
                    act.wait_ge(e0.hidden, 2 * e + k + 1)
                    if e >= 2:
                        act.wait_ge(e0.y, e - 1)
                    nc.scalar.activation(H0[:, e % 2, k, :], ps[:, 2 * (e % 2) + k, :], ACT.Silu).then_inc(e0.silu, 1)

            act.wait_ge(turned, 7)
            nc.scalar.copy(XTP[:, :, W:], ps[:, Y_BANK, :].rearrange("p (b t) -> p b t", b=B)).then_inc(turned_out, 1)
            act.wait_ge(a1.proj, 1)
            act.wait_ge(x1m.bq, 1)
            nc.scalar.activation(QT[:], ps[:, 0, :], ACT.Identity, bias=scaled_bq[:, 0:1],
                                 scale=DH ** -0.5).then_inc(a1.act_out, 1)
            act.wait_ge(a1.proj, 3)
            nc.scalar.copy(V[:].rearrange("p (b t) d -> p b (t d)", b=2), ps[:, 2:4, :]).then_inc(a1.act_out, 1)
            head_steps(a1)
            heads_out(a1, vec[:, 6:7])

            act.wait_ge(x1.proj, 2)
            nc.scalar.copy(V[:, 0:NT, :], ps[:, 2, :].rearrange("p (t d) -> p t d", t=NT)).then_inc(x1.act_out, 1)
            act.wait_ge(x1m.mean_ps, 1)
            nc.scalar.copy(MC[:], ps[:, 3, 0:B]).then_inc(x1m.mean, 1)
            act.wait_ge(x1m.value_ps, 1)
            nc.scalar.activation(MVB[:], ps[:, 4, 0:B], ACT.Identity, bias=vec[:, 9:10]).then_inc(x1m.value, 1)
            act.wait_ge(turned, 8)
            nc.scalar.copy(XT[:], ps[:, Y_BANK, :]).then_inc(turned_out, 1)
            act.wait_ge(x1.proj, 3)
            nc.scalar.activation(QT[:], ps[:, 0, :], ACT.Identity, bias=scaled_bq[:, 1:2],
                                 scale=DH ** -0.5).then_inc(x1.act_out, 1)
            head_steps(x1)
            heads_out(x1, vec[:, 9:10])

            act.wait_ge(turned, 9)
            nc.scalar.copy(XT[:], ps[:, Y_BANK, :]).then_inc(turned_out, 1)
            act.wait_ge(e1.low, 1)
            for t in range(NT):
                last = nc.scalar.activation(EX[:, t, :], ps[:, 4, t * E1:(t + 1) * E1], ACT.Exp, bias=NMX[:, t:t + 1],
                                            accum_out=SX[:, t:t + 1])
            last.then_inc(e1.ex, 1)
            act.wait_ge(e1.zh_ps, 1)
            nc.scalar.activation(ZG[:], ps[0:F1, 0:2, :], ACT.Silu).then_inc(e1.z_silu, 1)
            for g in range(0, 8, 2):
                act.wait_ge(e1.gather_ps, g + 1)
                nc.scalar.copy(XBT[:, :, 8 * g:8 * g + 8].rearrange("p e s -> p s e"),
                               ps[:, g % 4, :].rearrange("p (s e) -> p s e", s=8)).then_inc(e1.gather_act, 1)

            def pair(t, r):
                p = r % 2
                if not known(t) or t < PAIRS:
                    act.wait_ge(e1.hidden, t + 1)
                    if not known(t) or t >= 2:
                        act.wait_ge(e1.hg, t - 1)
                    nc.scalar.activation(GG[:, p, :], ps[0:F1, 2 + p, 0:2 * CAP], ACT.Silu).then_inc(e1.silu, 1)
                    act.wait_ge(e1.pw_t, t + 1)
                    if not known(t) or t >= 2:
                        act.wait_ge(e1.added, t - 1)
                    nc.scalar.copy(PM[:, p, :], ps[:, p, :]).then_inc(e1.pm, 1)
                if not known(t) or 1 <= t < PAIRS + 1:
                    q = 1 - p
                    act.wait_ge(e1.y, t)
                    if not known(t) or t >= 3:
                        act.wait_ge(e1.added, t - 2)
                    nc.scalar.copy(YS[:, q, :], ps[:, 4 + q, 0:P]).then_inc(e1.ys, 1)

            run_pairs(act, pair)

        @block.vector
        def _(dve):
            def norm(n, src, dst, eps):
                if n:
                    dve.wait_ge(ln_done, n)
                for t in range(NT):
                    last = nc.vector.bn_stats(st[:, t, :], src[:, t, :])
                last.then_inc(ln_chain, 1)
                dve.wait_ge(ln_chain, 2 * n + 1)
                for t in range(NT):
                    last = nc.vector.bn_aggr(mv[:, t, :], st[:, t, :])
                last.then_inc(ln_chain, 1)
                dve.wait_ge(ln_chain, 2 * n + 2)
                nc.vector.tensor_scalar(ve[:], mv[:, :, 1], eps, None, ALU.add).then_inc(ln_var, 1)
                dve.wait_ge(ln_rstd, n + 1)
                for t in range(NT):
                    last = nc.vector.tensor_scalar(dst[:, t, :], src[:, t, :], mv[:, t, 0:1], rstd[:, t:t + 1],
                                                   ALU.subtract, ALU.mult)
                last.then_inc(ln_done, 1)

            def head_steps(s, slopes=False):
                window = s.kind == "window"
                n_neg = 3 if s.kind == "padded" else 2

                def step(t, p):
                    if not known(t) or t < H:
                        dve.wait_ge(s.scores, t + 1)
                        if window:
                            nc.vector.tensor_tensor(NS[:, p, 0:512], cs[:, C_WIN:C_WIN + 512], ps[:, 2 * p, :],
                                                    ALU.subtract).then_inc(s.neg, 1)
                        else:
                            ns = NS[:, p, 0:2 * BLK].rearrange("p (b k) -> p b k", b=B)
                            sc = ps[:, 2 * p:2 * p + 2, 0:BLK]
                            if slopes:
                                rel = cs[:, C_REL:C_REL + BLK].unsqueeze(1).broadcast_to([P, B, BLK])
                                nc.vector.scalar_tensor_tensor(ns, rel, cs[:, ds(t + C_SL, 1)], sc,
                                                               ALU.mult, ALU.subtract).then_inc(s.neg, 1)
                            else:
                                nc.vector.tensor_tensor(ns, negrel[:], sc, ALU.subtract).then_inc(s.neg, 1)
                        dve.wait_ge(s.neg, t + 1)
                        last_sem = s.neg_chain if s.kind == "padded" else s.peak
                        if window:
                            nc.vector.tensor_reduce(NM[:, p, :], NS[:, p, 0:512].rearrange("p (k c) -> p k c", k=4),
                                                    AX, ALU.min).then_inc(last_sem, 1)
                        else:
                            to = MN if s.kind == "padded" else NM
                            nc.vector.tensor_reduce(to[:, p, 0::2], ns[:, :, 0:P], AX, ALU.min)
                            nc.vector.tensor_reduce(to[:, p, 1::2], ns[:, :, P:BLK], AX, ALU.min).then_inc(last_sem, 1)
                        if s.kind == "padded":
                            dve.wait_ge(s.neg_chain, t + 1)
                            nc.vector.tensor_scalar(NM[:, p, :], MN[:, p, :], peak_limit[:], None, ALU.min).then_inc(s.peak, 1)
                    if not known(t) or 1 <= t < H + 1:
                        q = 1 - p
                        dve.wait_ge(s.exps, t)
                        nc.vector.reciprocal(RI[:, q, :], RS[:, q, :]).then_inc(s.norm_chain, 1)
                        dve.wait_ge(s.norm_chain, t)
                        if window:
                            parts = [(k * P, P, k) for k in range(4)]
                        else:
                            parts = [(b * BLK + a, w, 2 * b + k) for b in range(B)
                                     for k, (a, w) in enumerate(((0, P), (P, 2 * P)))]
                        for a, w, k in parts:
                            last = nc.vector.tensor_scalar(PR[:, q, a:a + w], PR[:, q, a:a + w], RI[:, q, k:k + 1],
                                                           None, ALU.mult)
                        last.then_inc(s.probs, 1)
                    if (not known(t) or 2 <= t < H + 2) and not window:
                        dve.wait_ge(s.flipped, t - 1)
                        if not known(t) or t >= 4:
                            dve.wait_ge(s.heads, t - 3)
                        nc.vector.tensor_copy(PTS[:, p, BLK:2 * BLK], ps[:, PT_BANK + 1, 0:BLK]).then_inc(s.flip_dve, 1)

                run_steps(dve, H, step)

            dve.wait_ge(weff_ps, 1)
            dve.wait_ge(ld.w_a0, 16)
            nc.vector.scalar_tensor_tensor(wa0[:, 0:3, :], ps[:, 0, 0:3 * P].rearrange("p (k d) -> p k d", k=3), 2.0,
                                           wa0[:, 0:3, :], ALU.mult, ALU.add).then_inc(weff, 1)
            dve.wait_ge(a0.proj, 2)
            nc.vector.tensor_copy(KT[:, 0:N], ps[:, 2, :]).then_inc(a0.k_out, 1)
            dve.wait_ge(ld.ctx, 16)
            norm(0, C[:, 0:4], CN[:, 0:4], EPS_X)
            norm(1, C[:, 4:8], CN[:, 4:8], EPS_X)
            dve.wait_ge(ld.nkv, 16)
            nc.vector.tensor_scalar(nk2[:], cs[:, C_HALF:C_HALF + 2], nkv[:, 0:1], None, ALU.mult)
            nc.vector.tensor_scalar(nv16[:].rearrange("p c h -> p (c h)"), cs[:, C_NH:C_NH + P], nkv[:, 1:2], None,
                                    ALU.mult).then_inc(x0.null_w, 1)
            dve.wait_ge(ld.mask, 32)
            nc.vector.tensor_scalar(negpad[:], maskb[:, 0], -BIG, BIG, ALU.mult, ALU.add).then_inc(x0.negpad, 1)
            head_steps(a0, slopes=True)
            dve.wait_ge(a0.proj, 4)
            nc.vector.tensor_tensor(R[:], ps[:, Y_BANK, :].rearrange("p (t d) -> p t d", t=NT), X[:],
                                    ALU.add).then_inc(a0.resid, 1)
            dve.wait_ge(a0.resid, 1)
            norm(2, R, X, EPS_POST)

            dve.wait_ge(ln_done, 3)
            norm(3, X, XN, EPS_X)
            dve.wait_ge(x0.negpad, 1)

            def null_out(c, p):
                dve.wait_ge(x0.sn_ps, c + 1)
                nc.vector.tensor_copy(SN[:, p], ps[:, 2, 0:2 * NT].rearrange("p (t h) -> p t h", t=NT)
                                      ).then_inc(x0.sn, 1)

            def unit(c, cp, j, last_chunk=False):
                u, p = 4 * c + j, j % 2
                b = j // 2
                if not known(u) or u < 4 * XC:
                    if j == 0:
                        dve.wait_ge(x0.sn, c + 1)
                    dve.wait_ge(x0.scores, u + 1)
                    ns = NS[:, p, :].rearrange("p (k s) -> p k s", k=2)
                    null = SN[:, cp, 2 * b:2 * b + 2, p]
                    nc.vector.tensor_copy(NM[:, p, 0:2], null)
                    for k in range(2):
                        last = nc.vector.tensor_tensor_reduce(out=ns[:, k, :], in0=ps[:, 2 * p + k, :],
                                                              in1=negpad[:, b, :], scale=1.0, scalar=3e38,
                                                              op0=ALU.add, op1=ALU.min, accum_out=MN[:, p, k:k + 1])
                    last.then_inc(x0.neg, 1)
                    dve.wait_ge(x0.neg, u + 1)
                    nc.vector.tensor_tensor(NM[:, p, 0:2], MN[:, p, 0:2], NM[:, p, 0:2], ALU.min).then_inc(x0.low, 1)
                    dve.wait_ge(x0.low, u + 1)
                    nc.vector.tensor_tensor(DN[:, p, :], NM[:, p, 0:2], null, ALU.subtract).then_inc(x0.peak, 1)
                    if j == 3 and not last_chunk:
                        null_out(c + 1, 1 - cp)
                if not known(u) or 1 <= u < 4 * XC + 1:
                    q = 1 - p
                    pb, pc = ((j - 1) // 2, c) if j else (1, c - 1)
                    dve.wait_ge(x0.exps, u)
                    nc.vector.tensor_tensor(TS[:, q, :], RS[:, q, 0:2], PN[:, q, :], ALU.add).then_inc(x0.sums, 1)
                    dve.wait_ge(x0.sums, 2 * u - 1)
                    nc.vector.reciprocal(RI[:, q, 0:2], TS[:, q, :]).then_inc(x0.sums, 1)
                    dve.wait_ge(x0.sums, 2 * u)
                    dve.wait_ge(const_ready, 1)
                    nc.vector.tensor_tensor(PNN[:, 2 * pb:2 * pb + 2, ds(2 * pc + q, 1)], PN[:, q, :].unsqueeze(2),
                                            RI[:, q, 0:2].unsqueeze(2), ALU.mult)
                    for k in range(2):
                        last = nc.vector.tensor_scalar(PR[:, q, k * S2:(k + 1) * S2], PR[:, q, k * S2:(k + 1) * S2],
                                                       RI[:, q, k:k + 1], None, ALU.mult)
                    last.then_inc(x0.probs, 1)
                if not known(u) or 2 <= u < 4 * XC + 2:
                    dve.wait_ge(x0.flipped, u - 1)
                    if not known(u) or u >= 4:
                        dve.wait_ge(x0.heads, u - 3)
                    nc.vector.tensor_copy(PTS[:, p, 512:1024], ps[:, PT_BANK + 1, :]).then_inc(x0.flip_dve, 1)

            null_out(0, 0)
            for j in range(8):
                unit(j // 4, j // 4, j % 4)
            with dve.Fori(1, XC // 2 - 1) as i:
                for j in range(8):
                    unit(2 * i + j // 4, j // 4, j % 4)
            for j in range(8):
                unit(XC - 2 + j // 4, j // 4, j % 4, last_chunk=j >= 4)
            for j in range(2):
                unit(XC, 0, j)
            dve.wait_ge(x0.out, 1)
            norm(4, ps[:, Y_BANK, :].rearrange("p (t d) -> p t d", t=NT), XN, EPS_X)
            dve.wait_ge(ln_done, 5)
            dve.wait_ge(ld.vectors, 48)
            nc.vector.tensor_tensor(R[:], XN[:], row[:, 0, :].unsqueeze(1).broadcast_to([P, NT, P]),
                                    ALU.mult).then_inc(x0.affine, 1)
            dve.wait_ge(x0.affine, 1)
            dve.wait_ge(x0.base, 1)
            nc.vector.tensor_tensor(R[:], R[:], XB[:], ALU.add).then_inc(x0.affine, 1)
            dve.wait_ge(x0.affine, 2)
            norm(5, R, X, EPS_POST)

            chained = [0]

            def then(ins):
                chained[0] += 1
                ins.then_inc(e0.comb, 1)
                dve.wait_ge(e0.comb, chained[0])

            def by_expert(a):
                return a.unsqueeze(3).broadcast_to([P, NT, E0, E0])

            def by_rival(a):
                return a.unsqueeze(2).broadcast_to([P, NT, E0, E0])

            dve.wait_ge(e0.logits, 1)
            dve.wait_ge(ld.vectors, 48)
            nc.vector.tensor_tensor(Z0[:], ps[:, Y_BANK, 0:NT * E0].rearrange("p (t e) -> p t e", t=NT),
                                    grow[:, 0:E0].unsqueeze(1).broadcast_to([P, NT, E0]), ALU.add
                                    ).then_inc(e0.route, 1)
            dve.wait_ge(e0.ez, 1)
            then(nc.vector.tensor_scalar(EZ0[:], EZ0[:], 1.0, None, ALU.add))
            then(nc.vector.reciprocal(GS0[:], EZ0[:]))
            nc.vector.tensor_tensor(GT0[:], by_rival(GS0[:]), by_expert(GS0[:]), ALU.is_gt)
            then(nc.vector.tensor_tensor(EQ0[:], by_rival(GS0[:]), by_expert(GS0[:]), ALU.is_equal))
            then(nc.vector.tensor_tensor(EQ0[:].rearrange("p t a b -> p t (a b)"), EQ0[:].rearrange("p t a b -> p t (a b)"),
                                         cs[:, C_LT:C_ALL].unsqueeze(1).broadcast_to([P, NT, E0 * E0]), ALU.mult))
            then(nc.vector.tensor_tensor(GT0[:], GT0[:], EQ0[:], ALU.add))
            then(nc.vector.tensor_reduce(RK0[:], GT0[:], AX, ALU.add))
            then(nc.vector.scalar_tensor_tensor(SG0[:], RK0[:], K0 - 0.5, GS0[:], ALU.is_lt, ALU.mult))
            then(nc.vector.tensor_reduce(SM0[:], SG0[:], AX, ALU.add))
            then(nc.vector.tensor_scalar(SM0[:], SM0[:], 1e-6, None, ALU.add))
            then(nc.vector.reciprocal(IV0[:], SM0[:]))
            then(nc.vector.tensor_tensor(comb0[:], SG0[:], IV0[:].unsqueeze(2).broadcast_to([P, NT, E0]), ALU.mult))
            for e in range(E0):
                dve.wait_ge(e0.y, e + 1)
                if e:
                    dve.wait_ge(e0.acc, e)
                for t in range(NT):
                    last = nc.vector.scalar_tensor_tensor(R[:, t, :], ps[:, 4 + e % 2, t * P:(t + 1) * P],
                                                          comb0[:, t, e:e + 1], (R if e else X)[:, t, :],
                                                          ALU.mult, ALU.add)
                last.then_inc(e0.acc, 1)
            dve.wait_ge(e0.acc, E0)
            norm(6, R, X, EPS_POST)

            dve.wait_ge(ld.vectors, 48)
            nc.vector.tensor_scalar(scaled_bq[:, 0:1], vec[:, 4:5], DH ** -0.5, None, ALU.mult)
            nc.vector.tensor_scalar(scaled_bq[:, 1:2], vec[:, 7:8], DH ** -0.5, None, ALU.mult).then_inc(x1m.bq, 1)
            dve.wait_ge(pads, 1)
            dve.wait_ge(a1.proj, 2)
            nc.vector.tensor_scalar(KT[:].rearrange("p (b k) -> p b k", b=B)[:, :, W:],
                                    ps[:, 1, :].rearrange("p (b t) -> p b t", b=B), vec[:, 5:6], None,
                                    ALU.add).then_inc(a1.k_out, 1)
            head_steps(a1)
            dve.wait_ge(a1.proj, 4)
            dve.wait_ge(a1.bias_added, 1)
            nc.vector.tensor_tensor(R[:], ps[:, Y_BANK, :].rearrange("p (t d) -> p t d", t=NT), XB[:],
                                    ALU.add).then_inc(a1.resid, 1)
            dve.wait_ge(a1.resid, 1)
            norm(7, R, X, EPS_POST)

            shown = maskb[:, 1, :, 0:T]
            nc.vector.tensor_reduce(all_out[:], shown, mybir.AxisListType.XY, ALU.min).then_inc(x1m.flag, 1)
            dve.wait_ge(x1m.flag, 1)
            nc.vector.tensor_scalar(peak_limit[:], all_out[:], BIG * 1e6, 1e20, ALU.mult, ALU.add).then_inc(x1m.flag, 1)
            nc.vector.tensor_scalar(negrel[:], cs[:, C_REL:C_REL + BLK].unsqueeze(1).broadcast_to([P, B, BLK]),
                                    -1e20, BIG, ALU.is_le, ALU.mult).then_inc(x1m.rel, 1)
            dve.wait_ge(x1m.rel, 1)
            nc.vector.scalar_tensor_tensor(negrel[:, :, 0:P], shown[:, :, 0:P], BIG, negrel[:, :, 0:P],
                                           ALU.mult, ALU.add)
            nc.vector.scalar_tensor_tensor(negrel[:, :, P:BLK], shown, BIG, negrel[:, :, P:BLK],
                                           ALU.mult, ALU.add).then_inc(x1m.rel, 1)
            dve.wait_ge(x1.proj, 1)
            nc.vector.tensor_scalar(KT[:, 0:N], ps[:, 1, :], vec[:, 8:9], None, ALU.add).then_inc(x1.k_out, 1)
            dve.wait_ge(x1m.rel, 2)
            dve.wait_ge(x1m.flag, 2)
            head_steps(x1)
            dve.wait_ge(x1.act_out, 3)
            dve.wait_ge(x1m.flag, 1)
            nc.vector.copy_predicated(OT[:].rearrange("p (b t) -> p b t", b=B),
                                      all_out[:].bitcast(mybir.dt.uint32).unsqueeze(2).broadcast_to([P, B, T]),
                                      MVB[:].unsqueeze(2).broadcast_to([P, B, T])).then_inc(x1m.patched, 1)
            dve.wait_ge(x1.proj, 4)
            dve.wait_ge(x1.bias_added, 1)
            nc.vector.tensor_tensor(R[:], ps[:, Y_BANK, :].rearrange("p (t d) -> p t d", t=NT), XB[:],
                                    ALU.add).then_inc(x1.resid, 1)
            dve.wait_ge(x1.resid, 1)
            norm(8, R, X, EPS_POST)

            def each(a):
                return a.unsqueeze(2).broadcast_to([P, NT, E1])

            chosen = [0]

            def then1(ins):
                chosen[0] += 1
                ins.then_inc(e1.sel, 1)
                dve.wait_ge(e1.sel, chosen[0])

            dve.wait_ge(e1.logits, 1)
            then1(nc.vector.tensor_reduce(MX[:], ps[:, 4, 0:NT * E1].rearrange("p (t e) -> p t e", t=NT), AX, ALU.max))
            nc.vector.tensor_scalar(NMX[:], MX[:], -1.0, None, ALU.mult).then_inc(e1.low, 1)
            dve.wait_ge(ln_done, 9)
            nc.vector.tensor_copy(XH[:], X[:]).then_inc(e1.parts, 1)
            dve.wait_ge(e1.parts, 1)
            nc.vector.tensor_tensor(XL[:], X[:], XH[:], ALU.subtract).then_inc(e1.parts, 1)
            dve.wait_ge(e1.ex, 1)
            then1(nc.vector.reciprocal(MX[:], SX[:]))
            then1(nc.vector.tensor_tensor(SC[:], EX[:], each(MX[:]), ALU.mult))
            then1(nc.vector.tensor_tensor(SB[:], SC[:], grow[:, E0:].unsqueeze(1).broadcast_to([P, NT, E1]), ALU.add))
            for t in range(NT):
                last = nc.vector.max(T8[:, t, :], SB[:, t, :])
            then1(last)
            sixth = each(T8[:, :, K1 - 1])
            dve.wait_ge(const_ready, 1)
            nc.vector.tensor_tensor(EQM[:], SB[:], sixth, ALU.is_equal)
            nc.vector.tensor_tensor(SCAN[:, 0, :, LEAD:], SB[:], sixth, ALU.is_equal)
            then1(nc.vector.tensor_tensor(GTM[:], SB[:], sixth, ALU.is_gt))
            then1(nc.vector.tensor_reduce(ROOM[:], GTM[:], AX, ALU.add))
            then1(nc.vector.tensor_scalar(ROOM[:], ROOM[:], -1.0, float(K1), ALU.mult, ALU.add))
            for k in range(6):
                a, z = SCAN[:, k % 2], SCAN[:, 1 - k % 2]
                then1(nc.vector.tensor_tensor(z[:, :, LEAD:], a[:, :, LEAD:], a[:, :, LEAD - 2 ** k:LEAD + E1 - 2 ** k],
                                              ALU.add))
            then1(nc.vector.tensor_tensor(SEL[:], SCAN[:, 0, :, LEAD:], each(ROOM[:]), ALU.is_le))
            then1(nc.vector.tensor_tensor(SEL[:], SEL[:], EQM[:], ALU.mult))
            then1(nc.vector.tensor_tensor(SEL[:], SEL[:], GTM[:], ALU.add))
            then1(nc.vector.tensor_copy(SELh[:], SEL[:]))
            then1(nc.vector.tensor_tensor(WT[:], SEL[:], SC[:], ALU.mult))
            assert chosen[0] == SEL_DONE, chosen
            dve.wait_ge(e1.z_silu, 1)
            nc.vector.tensor_tensor(ZH[:], ZG[:], ps[0:F1, 2:4, :], ALU.mult).then_inc(e1.z_mult, 1)
            dve.wait_ge(e1.count_ps, 1)
            nc.vector.tensor_tensor(QS[:], ps[:, 5, 0:NT * E1].rearrange("p (t e) -> p t e", t=NT), SEL[:],
                                    ALU.mult).then_inc(e1.queue, 1)
            dve.wait_ge(e1.queue, 1)
            dve.wait_ge(ld.halfs, 16)
            for t in range(NT):
                nc.vector.tensor_tensor(PH[:, t], hs[:, G_SLOT:G_SLOT + E1 * CAP].rearrange("p (s e) -> p s e", e=E1),
                                        QS[:, t, :].unsqueeze(1).broadcast_to([P, CAP, E1]),
                                        ALU.is_equal).then_inc(e1.onehot, 1)
            for g in range(1, 8, 2):
                dve.wait_ge(e1.gather_ps, g + 1)
                nc.vector.tensor_copy(XBT[:, :, 8 * g:8 * g + 8].rearrange("p e s -> p s e"),
                                      ps[:, g % 4, :].rearrange("p (s e) -> p s e", s=8)).then_inc(e1.gather_dve, 1)

            def pair(t, r):
                p = r % 2
                if not known(t) or t < PAIRS:
                    if not known(t) or t >= 2:
                        dve.wait_ge(e1.pw_t, t - 1)
                    nc.vector.tensor_tensor(PW[:, p].rearrange("p t (e s) -> p t e s", e=2),
                                            PH[:, :, :, ds(2 * t, 2)].rearrange("p t s e -> p t e s"),
                                            WT[:, :, ds(2 * t, 2)].unsqueeze(3).broadcast_to([P, NT, 2, CAP]),
                                            ALU.mult).then_inc(e1.pw, 1)
                    dve.wait_ge(e1.hidden, t + 1)
                    dve.wait_ge(e1.silu, t + 1)
                    if not known(t) or t >= 2:
                        dve.wait_ge(e1.y, t - 1)
                    nc.vector.tensor_tensor(HG[:, p, :], GG[:, p, :], ps[0:F1, 2 + p, 2 * CAP:4 * CAP],
                                            ALU.mult).then_inc(e1.hg, 1)

            run_pairs(dve, pair)
            dve.wait_ge(e1.added, PAIRS)
            nc.vector.tensor_tensor(R[:], ps[:, O_BANK, :].rearrange("p (t d) -> p t d", t=NT), X[:],
                                    ALU.add).then_inc(e1.router, 1)
            dve.wait_ge(e1.router, 1)
            norm(9, R, X, EPS_POST)


def kernel(**inputs):
    import concourse.bacc as bacc
    from concourse.bass_utils import run_bass_kernel_spmd

    def a(name):
        return np.asarray(inputs[name])

    def t(name):
        return a(name).T

    consts, halfs = shape_constants()
    zeros = np.zeros
    arrays = {
        "x": a("x").reshape(N, P),
        "ctx": a("ctx_1024").reshape(B * S2, P),
        "mask_x0": a("mask_BxS2_bf1").view(np.uint32).reshape(1, B, S2 // 4),
        "mask_x1": a("mask_BxS2_bk0").view(np.uint32).reshape(1, B, S2 // 4),
        "consts": consts,
        "halfs": halfs,
        "cols": np.stack([a(n) for n in ("L0_xattn_ln1_s", "L0_xattn_ln1_b", "L0_xattn_lnc_s", "L0_xattn_lnc_b",
                                         "L1_attn_bq", "L1_attn_bk", "L1_attn_bv",
                                         "L1_xattn_bq", "L1_xattn_bk", "L1_xattn_bv")], 1),
        "rows": np.stack([a(n) for n in ("L0_xattn_lno_s", "L0_xattn_lno_b", "L1_attn_bo", "L1_xattn_bo")])[None],
        "gate_rows": np.concatenate([a("L0_ffn_balance_bias"), a("L1_ffn_gate_b")])[None],
        "lora": np.stack([a("L0_attn_Bq"), a("L0_attn_Bk"), a("L0_attn_Bv"),
                          t("L0_attn_Aq"), t("L0_attn_Ak"), t("L0_attn_Av")], 1),
        "w_a0": np.stack([t("L0_attn_Wq"), t("L0_attn_Wk"), t("L0_attn_Wv"), t("L0_attn_Wp")], 1),
        "w_x0": np.stack([a("L0_xattn_Wq").reshape(P, XC, P).transpose(1, 0, 2),
                          a("L0_xattn_Wkv")[:, :XC * P].reshape(P, XC, P).transpose(1, 0, 2),
                          a("L0_xattn_Wkv")[:, XC * P:].reshape(P, XC, P).transpose(1, 0, 2)], 2),
        "wo_x0": a("L0_xattn_Wo").reshape(XC, P, P).transpose(1, 0, 2),
        "null_kv": np.concatenate([t("L0_xattn_null_kv")] * 2),
        "gate0": t("L0_ffn_gate_w"),
        "w_e0": np.stack([a("L0_ffn_w1").transpose(2, 0, 1),
                          a("L0_ffn_w2").reshape(E0, P, 2, P).transpose(3, 0, 2, 1).reshape(P, E0, F0)], 2),
        "w_a1": np.stack([t("L1_attn_Wq"), t("L1_attn_Wk"), t("L1_attn_Wv"), t("L1_attn_Wo")], 1),
        "w_x1": np.stack([a("L1_xattn_Wq"), a("L1_xattn_Wk"), a("L1_xattn_Wv"), a("L1_xattn_Wo")], 1),
        "gate1": t("L1_ffn_gate_w"),
        "w13_e1": np.stack([a("L1_ffn_w1"), a("L1_ffn_w3")], 1).reshape(E1 // 2, 4, F1, P).transpose(0, 3, 1, 2),
        "w2_e1": a("L1_ffn_w2").reshape(E1 // 2, 2, P, F1).transpose(0, 3, 1, 2),
        "ws13": np.stack([a("L1_ffn_ws1"), a("L1_ffn_ws3")]).reshape(4, F1, P).transpose(2, 0, 1),
        "ws2": a("L1_ffn_ws2").reshape(P, 2, F1).transpose(2, 1, 0),
    }
    nc = bacc.Bacc("TRN2", target_bir_lowering=False, num_devices=1)
    args = []
    for name, v in arrays.items():
        arrays[name] = v = np.ascontiguousarray(v)
        args.append(nc.dram_tensor(f"in_{name}", v.shape, mybir.dt.from_np(v.dtype), kind="ExternalInput").ap())
    result = nc.dram_tensor("out_0", (N, P), F32, kind="ExternalOutput").ap()
    decoder(nc, *args, result)
    r = run_bass_kernel_spmd(nc, [{f"in_{k}": v for k, v in arrays.items()}], core_ids=[0])
    return np.asarray(r.results[0]["out_0"]).reshape(B, T, P)
```

```python
from contextlib import ExitStack

import numpy as np

import concourse.bass as bass
from concourse import mybir

P = 128
B, T, S2 = 2, 256, 512
N = B * T
NT = N // P
H = 16
DH = P // H
XC = 8
XD = 64
E0, F0, K0 = 8, 256, 2
E1, F1, K1, CAP = 64, 88, 6, 64
W = 64
PAD = T + W
EPS_POST, EPS_X = 1e-5, 1e-6
BIG = 1e30
BLK = 384

F32, F16, BF16, U8 = mybir.dt.float32, mybir.dt.float16, mybir.dt.bfloat16, mybir.dt.uint8
ALU = mybir.AluOpType
ACT = mybir.ActivationFunctionType
AX = mybir.AxisListType.X
ds = bass.ds

COLS = ["ln1_s", "ln1_b", "lnc_s", "lnc_b", "a1_bq", "a1_bk", "a1_bv", "x1_bq", "x1_bk", "x1_bv"]
ROWS = ["lno_s", "lno_b", "a1_bo", "x1_bo"]
C_ID, C_HM, C_SL, C_REL, C_WIN, C_NH, C_HALF, C_LT = 0, 128, 144, 162, 546, 1058, 1314, 1316
C_ALL = C_LT + E0 * E0
G_CUM, G_ONE, G_ID, G_SLOT = 0, 128, 640, 768
G_ALL = G_SLOT + E1 * CAP
V_UP, PR_UP = 64.0, 2048.0


def shape_constants():
    p = np.arange(P)
    c = np.zeros((P, C_ALL), np.float32)
    c[:, C_ID:C_ID + P] = np.eye(P)
    c[:, C_HM:C_HM + H] = p[:, None] // DH == np.arange(H)
    start = 2.0 ** -0.5
    c[:, C_SL:C_SL + H] = -np.float32(start * start ** np.arange(H))
    j = np.arange(P)
    near = np.where(j[None] <= p[:, None], p[:, None] - j[None], -1e34)
    c[:, C_REL:C_REL + BLK] = np.concatenate([near, p[:, None] - j[None] + P, near], 1)
    win = np.zeros((P, 4, P), np.float32)
    win[:W, 0::2, :W] = 1e9
    c[:, C_WIN:C_WIN + 512] = win.reshape(P, 512)
    c[:XD, C_NH:C_NH + H * H] = np.eye(H).reshape(1, H * H)
    c[:, C_HALF:C_HALF + 2] = p[:, None] // XD == np.arange(2)
    c[:, C_LT:C_ALL] = (np.arange(E0)[None] < np.arange(E0)[:, None]).reshape(1, E0 * E0)
    g = np.zeros((P, G_ALL), np.float16)
    g[:, G_CUM:G_CUM + P] = p[:, None] <= j[None]
    g[:, G_ONE:G_ONE + 512] = 1
    g[:, G_ID:G_ID + P] = np.eye(P)
    g[:, G_SLOT:G_SLOT + E1 * CAP] = np.arange(E1 * CAP)[None] // E1 + 1
    return c, g


def decoder(nc, x, ctx, mask_x0, mask_x1, consts, halfs, cols, rows, gate_rows, lora, w_a0, w_x0, wq_t_x0, wo_x0, null_kv,
            gate0, w_e0, w_a1, w_x1, gate1, w13_e1, w2_e1, ws13, ws2, out):
    with ExitStack() as stack:
        def sb(name, shape, dt=F32):
            return stack.enter_context(nc.sbuf_tensor(name, shape, dt))

        def sem(name):
            return stack.enter_context(nc.semaphore(name))

        ps = stack.enter_context(nc.psum_tensor("ps", [P, 8, 512], F32))
        PT_BANK, O_BANK, Y_BANK = 4, 6, 7

        cs = sb("cs", [P, C_ALL])
        hs = sb("hs", [P, G_ALL], F16)
        vec = sb("vec", [P, len(COLS)])
        row = sb("row", [P, len(ROWS), P])
        grow = sb("grow", [P, E0 + E1])
        ident = cs[:, C_ID:C_ID + P]
        ident16 = hs[:, G_ID:G_ID + P]
        lora_sb = sb("lora_sb", [8, 6, P])
        wa0 = sb("wa0", [P, 4, P])
        wa1 = sb("wa1", [P, 4, P])
        wx1 = sb("wx1", [P, 4, P])
        x0ring = sb("x0ring", [P, 2, 3, P])
        nkv = sb("nkv", [P, 2])
        wo_all = sb("wo_all", [P, H, P])
        g0w = sb("g0w", [P, E0])
        g1w = sb("g1w", [P, E1])
        e0w = sb("e0w", [P, E0, 2, F0])
        ws13_sb = sb("ws13_sb", [P, 4, F1])
        ws2_sb = sb("ws2_sb", [F1, 2, P])
        RING = 4
        w13r = sb("w13r", [P, RING, 4, F1])
        w2r = sb("w2r", [F1, RING, 2, P])
        mask_words = sb("mask_words", [P, 2, B, S2 // 4], mybir.dt.uint32)
        maskb = mask_words[:].bitcast(U8)

        X = sb("X", [P, NT, P])
        XB = sb("XB", [P, NT, P])
        R = sb("R", [P, NT, P])
        XT = sb("XT", [P, N])
        XN = sb("XN", [P, NT, P])
        XTP = sb("XTP", [P, B, PAD])
        C = sb("C", [P, 8, P])
        CN = sb("CN", [P, 8, P])
        CNT = sb("CNT", [P, B * S2])
        CT = sb("CT", [P, N])
        QT = sb("QT", [P, N])
        KT = sb("KT", [P, B * PAD])
        V = sb("V", [P, 8, P])
        OT = sb("OT", [P, N])
        Kh = sb("Kh", [P, 2, B * PAD])
        VM = P + 16
        Vh = sb("Vh", [P, 2, 8, VM])
        region = sb("region", [P, 8192])

        def part_of(buffer, first, **sizes):
            names = " ".join(sizes)
            width = int(np.prod(list(sizes.values())))
            return buffer[:, first:first + width].rearrange(f"p ({names}) -> p {names}", **sizes)

        NS = part_of(region, 0, i=2, c=1024)
        PR = part_of(region, 2048, i=2, c=1024)
        PTS = part_of(region, 4096, i=2, c=1024)
        NM = sb("NM", [P, 2, 4])
        MN = sb("MN", [P, 2, 4])
        RS = sb("RS", [P, 2, 4])
        RI = sb("RI", [P, 2, 4])
        zero = sb("zero", [P, 512])
        mhalf = sb("mhalf", [P, 4])
        zcol = sb("zcol", [P, 1])
        st = sb("st", [P, 4, 6])
        mv = sb("mv", [P, 4, 2])
        ve = sb("ve", [P, 4])
        rstd = sb("rstd", [P, 4])
        negpad = sb("negpad", [P, B, S2])
        negrel = sb("negrel", [P, B, BLK])

        zh = sb("zh", [P, P], F16)
        gate = sb("gate", [P, 2])
        region2 = sb("region2", [P, 5120])
        QC = (part_of(region2, 0, h=2, c=N), part_of(CN[:].rearrange("p t d -> p (t d)"), 0, h=2, c=N))
        KC = part_of(region2, 1024, i=2, c=B * S2)
        VC = region2[:, 3072:5120].bitcast(F16).rearrange("p (i t h two d) -> p i t h two d", i=2, t=8, h=2, two=2)
        PRH, PRL = (region[:, 6144 + 1024 * k:7168 + 1024 * k].bitcast(F16).rearrange("p (i c) -> p i c", i=2)
                    for k in range(2))
        PTH, PTL = (region[:, 4096 + 1024 * k:5120 + 1024 * k].bitcast(F16).rearrange("p (i c) -> p i c", i=2)
                    for k in range(2))
        VF = part_of(Kh[:].rearrange("p i k -> p (i k)"), 0, t=8, h=2, d=XD)
        PT16 = ps[:, PT_BANK:PT_BANK + 2, :].bitcast(F16)
        OC = sb("OC", [P, 2, 2, N])
        nk2 = sb("nk2", [P, 2])
        nv16 = part_of(region, 6144, a=H, b=H)
        nvo = sb("nvo", [H, P])
        wqt = part_of(region, 6400, c=XC, d=P)
        WN = sb("WN", [P, H])
        SN = sb("SN", [P, NT, H])
        DN = sb("DN", [P, 2, 2])
        PN = sb("PN", [P, 2, 2])
        TS = sb("TS", [P, 2, 2])
        PNN = sb("PNN", [P, NT, H])
        PNT = sb("PNT", [H, N])
        Z0 = sb("Z0", [P, NT, E0])
        EZ0 = sb("EZ0", [P, NT, E0])
        GS0 = sb("GS0", [P, NT, E0])
        GT0 = sb("GT0", [P, NT, E0, E0])
        EQ0 = sb("EQ0", [P, NT, E0, E0])
        RK0 = sb("RK0", [P, NT, E0])
        SG0 = sb("SG0", [P, NT, E0])
        SM0 = sb("SM0", [P, NT])
        IV0 = sb("IV0", [P, NT])
        comb0 = sb("comb0", [P, NT, E0])
        H0 = part_of(region, 6144, i=2, k=2, c=N)
        all_out = sb("all_out", [P, 1])
        peak_limit = sb("peak_limit", [P, 1])
        MC = sb("MC", [P, B])
        MVB = sb("MVB", [P, B])
        scaled_bq = sb("scaled_bq", [P, 2])
        mean_col = sb("mean_col", [P, 1])
        CNf = CN[:].rearrange("p t d -> p (t d)")
        npf = negpad[:].rearrange("p b s -> p (b s)")
        MX = sb("MX", [P, NT])
        NMX = sb("NMX", [P, NT])
        SX = sb("SX", [P, NT])
        EX = part_of(CNf, 0, t=NT, e=E1)
        SC = part_of(CNf, 256, t=NT, e=E1)
        SB = part_of(CNf, 512, t=NT, e=E1 + 2)
        T8 = sb("T8", [P, NT, 8])
        MARK = 1e38
        RP = sb("RP", [P, NT, E1 + 2])
        SEL = part_of(npf, 256, t=NT, e=E1)
        SELh = sb("SELh", [P, NT, E1], F16)
        WT = part_of(npf, 512, t=NT, e=E1)
        XH = sb("XH", [P, NT, P], F16)
        XL = sb("XL", [P, NT, P], F16)
        QS = sb("QS", [P, NT, E1], F16)
        PH = region[:].bitcast(F16).rearrange("p (t s e) -> p t s e", t=NT, s=CAP)
        XBT = part_of(region2, 0, e=E1, s=CAP)
        e0f = e0w[:].rearrange("p e k f -> p (e k f)")
        ZG = part_of(e0f[0:F1, :], 0, k=2, n=N)
        ZH = part_of(e0f[0:F1, :], 1024, k=2, n=N)
        PM = part_of(e0f, 2048, i=RING, n=N)
        GG = sb("GG", [F1, 2, 2 * CAP])
        HG = sb("HG", [F1, 2, 2 * CAP])
        PW = sb("PW", [P, 2, NT, 2 * CAP])
        YS = sb("YS", [P, 2, P])

        class ld:
            x = sem("load_x")
            consts = sem("load_consts")
            more_consts = sem("load_more_consts")
            halfs = sem("load_halfs")
            lora = sem("load_lora")
            w_a0 = sem("load_w_a0")
            nkv = sem("load_nkv")
            ctx = sem("load_ctx")
            vectors = sem("load_vectors")
            mask = sem("load_mask")
            wo_all = sem("load_wo_all")
            gate0 = sem("load_gate0")
            w_e0 = sem("load_w_e0")
            w_a1 = sem("load_w_a1")
            late = sem("load_late")
        const_ready = sem("const_ready")
        ln_chain = sem("ln_chain")
        ln_var = sem("ln_var")
        ln_rstd = sem("ln_rstd")
        ln_done = sem("ln_done")
        turned = sem("turned")
        turned_out = sem("turned_out")
        weff_ps, weff = sem("weff_ps"), sem("weff")

        class HeadSignals:
            def __init__(self, tag, kind):
                self.kind = kind
                self.proj = sem(tag + "_proj")
                self.act_out = sem(tag + "_act_out")
                self.k_out = sem(tag + "_k_out")
                self.kh_ready = sem(tag + "_kh_ready")
                self.vh_ready = sem(tag + "_vh_ready")
                self.pool_chain = sem(tag + "_pool_chain")
                self.scores = sem(tag + "_scores")
                self.neg = sem(tag + "_neg")
                self.peak = sem(tag + "_peak")
                self.exps = sem(tag + "_exps")
                self.norm_chain = sem(tag + "_norm_chain")
                self.probs = sem(tag + "_probs")
                self.flipped = sem(tag + "_flipped")
                self.flip_act = sem(tag + "_flip_act")
                self.heads = sem(tag + "_heads")
                self.resid = sem(tag + "_resid")
                if kind != "window":
                    self.flip_dve = sem(tag + "_flip_dve")
                if kind == "causal":
                    self.rel = sem(tag + "_rel")
                if kind != "causal":
                    self.bias_added = sem(tag + "_bias_added")

        a0 = HeadSignals("a0", "causal")
        a1 = HeadSignals("a1", "window")
        x1 = HeadSignals("x1", "padded")
        NORMS = 10
        stored = sem("stored")

        class x0:
            q_ps = sem("x0_q_ps")
            k_ps = sem("x0_k_ps")
            v_ps = sem("x0_v_ps")
            sn_ps = sem("x0_sn_ps")
            q = sem("x0_q")
            k = sem("x0_k")
            v = sem("x0_v")
            v_high = sem("x0_v_high")
            v_parts = sem("x0_v_parts")
            high = sem("x0_high")
            sn = sem("x0_sn")
            oc = sem("x0_oc")
            scores = sem("x0_scores")
            neg = sem("x0_neg")
            low = sem("x0_low")
            peak = sem("x0_peak")
            exps = sem("x0_exps")
            sums = sem("x0_sums")
            probs = sem("x0_probs")
            flipped = sem("x0_flipped")
            flip_act = sem("x0_flip_act")
            flip_dve = sem("x0_flip_dve")
            heads = sem("x0_heads")
            w_even = sem("x0_w_even")
            w_odd = sem("x0_w_odd")
            null_w = sem("x0_null_w")
            nvo_ps = sem("x0_nvo_ps")
            nvo = sem("x0_nvo")
            pnt_ps = sem("x0_pnt_ps")
            pnt = sem("x0_pnt")
            out = sem("x0_out")
            affine = sem("x0_affine")
            base = sem("x0_base")
            negpad = sem("x0_negpad")
        class e0:
            logits = sem("e0_logits")
            route = sem("e0_route")
            ez = sem("e0_ez")
            comb = sem("e0_comb")
            hidden = sem("e0_hidden")
            silu = sem("e0_silu")
            y = sem("e0_y")
            acc = sem("e0_acc")

        SEL_DONE = 10
        LAST = 3

        def run_steps(eng, steps, step, before=4, unroll=2):
            for t in range(before):
                step(t, t % 2)
            with eng.Fori(before // unroll, steps // unroll) as i:
                for k in range(unroll):
                    step(unroll * i + k, k % 2)
            for t in range(steps, steps + LAST):
                step(t, t % 2)

        def run_pairs(eng, pair, ahead=0):
            for t in range(RING):
                pair(t, t)
            with eng.Fori(1, PAIRS // RING - ahead) as i:
                for r in range(RING):
                    pair(RING * i + r, r)
            for t in range(PAIRS - RING * ahead, PAIRS + 2):
                pair(t, t % RING)

        def known(t):
            return isinstance(t, int)

        class x1m:
            flag = sem("x1m_flag")
            rel = sem("x1m_rel")
            mean_ps = sem("x1m_mean_ps")
            mean = sem("x1m_mean")
            value_ps = sem("x1m_value_ps")
            value = sem("x1m_value")
            patched = sem("x1m_patched")
            bq = sem("x1m_bq")
        pads = sem("pads")
        class e1:
            logits = sem("e1_logits")
            router = sem("e1_router")
            low = sem("e1_low")
            ex = sem("e1_ex")
            sel = sem("e1_sel")
            count_ps = sem("e1_count_ps")
            queue = sem("e1_queue")
            parts = sem("e1_parts")
            onehot = sem("e1_onehot")
            gather_ps = sem("e1_gather_ps")
            gather_act = sem("e1_gather_act")
            zh_ps = sem("e1_zh_ps")
            z_silu = sem("e1_z_silu")
            z_mult = sem("e1_z_mult")
            pw = sem("e1_pw")
            pw_t = sem("e1_pw_t")
            pm = sem("e1_pm")
            hidden = sem("e1_hidden")
            silu = sem("e1_silu")
            hg = sem("e1_hg")
            y = sem("e1_y")
            ys = sem("e1_ys")
            added = sem("e1_added")
            w0 = sem("e1_w0")
            w1 = sem("e1_w1")
            w2 = sem("e1_w2")
            w3 = sem("e1_w3")
        PAIRS = E1 // 2

        block = stack.enter_context(nc.Block())

        @block.sync
        def _(sp):
            sp.dma_start(X[:], x.rearrange("(t p) d -> p t d", p=P)).then_inc(ld.x, 16)
            sp.dma_start(lora_sb[:], lora).then_inc(ld.lora, 16)
            sp.dma_start(cs[:, 0:C_WIN], consts[:, 0:C_WIN]).then_inc(ld.consts, 16)
            sp.dma_start(wa0[:], w_a0).then_inc(ld.w_a0, 16)
            sp.dma_start(cs[:, C_WIN:], consts[:, C_WIN:]).then_inc(ld.more_consts, 16)
            sp.dma_start(vec[:], cols).then_inc(ld.vectors, 16)
            sp.dma_start(row[:], rows.broadcast_to([P, len(ROWS), P])).then_inc(ld.vectors, 16)
            sp.dma_start(grow[:], gate_rows.broadcast_to([P, E0 + E1])).then_inc(ld.vectors, 16)
            sp.dma_start(mask_words[:, 0], mask_x0.broadcast_to([P, B, S2 // 4])).then_inc(ld.mask, 16)
            sp.dma_start(mask_words[:, 1], mask_x1.broadcast_to([P, B, S2 // 4])).then_inc(ld.mask, 16)
            sp.dma_start(hs[:, 0:G_SLOT], halfs[:, 0:G_SLOT]).then_inc(ld.halfs, 16)
            sp.dma_start(hs[:, G_SLOT:], halfs[:, G_SLOT:]).then_inc(ld.late, 16)
            sp.dma_start(nkv[:], null_kv).then_inc(ld.nkv, 16)
            sp.dma_start(wqt, wq_t_x0).then_inc(ld.wo_all, 16)
            sp.dma_start(wo_all[:], wo_x0).then_inc(ld.wo_all, 16)
            sp.dma_start(g0w[:], gate0).then_inc(ld.gate0, 16)
            sp.dma_start(e0w[:], w_e0).then_inc(ld.w_e0, 16)
            sp.dma_start(wa1[:], w_a1).then_inc(ld.w_a1, 16)
            sp.dma_start(wx1[:], w_x1).then_inc(ld.late, 16)
            sp.dma_start(g1w[:], gate1).then_inc(ld.late, 16)
            sp.dma_start(ws13_sb[:], ws13).then_inc(ld.late, 16)
            sp.dma_start(ws2_sb[:], ws2).then_inc(ld.late, 16)
            sp.dma_start(x0ring[:, 0], w_x0[0]).then_inc(x0.w_even, 16)
            sp.dma_start(x0ring[:, 1], w_x0[1]).then_inc(x0.w_odd, 16)
            with sp.Fori(1, XC // 2) as i:
                for k, arrived in ((0, x0.w_even), (1, x0.w_odd)):
                    sp.wait_ge(x0.v_ps, 2 * i + k - 1)
                    sp.dma_start(x0ring[:, k], w_x0[ds(2 * i + k, 1)].rearrange("a p k d -> (a p) k d")).then_inc(arrived, 16)
            ring_full = (e1.w0, e1.w1, e1.w2, e1.w3)
            for r in range(RING):
                sp.dma_start(w13r[:, r], w13_e1[r]).then_inc(ring_full[r], 16)
                sp.dma_start(w2r[:, r], w2_e1[r]).then_inc(ring_full[r], 16)
            with sp.Fori(1, PAIRS // RING) as i:
                for r in range(RING):
                    sp.wait_ge(e1.y, RING * i + r - RING + 1)
                    sp.dma_start(w13r[:, r], w13_e1[ds(RING * i + r, 1)].rearrange("a p k d -> (a p) k d")
                                 ).then_inc(ring_full[r], 16)
                    sp.dma_start(w2r[:, r], w2_e1[ds(RING * i + r, 1)].rearrange("a p k d -> (a p) k d")
                                 ).then_inc(ring_full[r], 16)
            tiles_out = out.rearrange("(t p) d -> p t d", p=P)
            for half in range(2):
                sp.wait_ge(ln_done, NT * (NORMS - 1) + 2 * half + 2)
                sp.dma_start(tiles_out[:, 2 * half:2 * half + 2], X[:, 2 * half:2 * half + 2]).then_inc(stored, 16)
            sp.wait_ge(stored, 32)

        @block.gpsimd
        def _(pool):
            nc.gpsimd.memset(zero[:], 0.0)
            nc.gpsimd.memset(mhalf[:], -0.5)
            nc.gpsimd.memset(zcol[:], 0.0)
            nc.gpsimd.memset(zh[:], 0.0)
            nc.gpsimd.memset(mean_col[:], 1.0 / S2)
            nc.gpsimd.memset(Vh[:], 0.0)
            nc.gpsimd.memset(QC[0], 0.0)
            nc.gpsimd.memset(XTP[:], 0.0).then_inc(const_ready, 1)
            pool.wait_ge(ld.consts, 16)

            def root(n):
                pool.wait_ge(const_ready, 1)
                pool.wait_ge(ln_var, n + 1)
                nc.gpsimd.tensor_tensor(rstd[:], ve[:], mhalf[:], ALU.pow).then_inc(ln_rstd, 1)

            def masked_heads(s):
                window = s.kind == "window"
                width = B * PAD if window else N
                tiles = 8 if window else NT
                pool.wait_ge(s.k_out, 1)
                pool.wait_ge(s.act_out, 2)
                pool.wait_ge(const_ready, 1)

                def keys(t, p):
                    if not known(t) or t >= 2:
                        pool.wait_ge(s.scores, t - 1)
                        pool.wait_ge(const_ready, 1)
                    nc.gpsimd.tensor_tensor(Kh[:, p, 0:width], KT[:, 0:width],
                                            cs[:, ds(t + C_HM, 1)].broadcast_to([P, width]),
                                            ALU.mult).then_inc(s.kh_ready, 1)

                def step(t, p, more_keys=True):
                    if more_keys:
                        keys(t + 1, 1 - p)
                    if not known(t) or t >= 2:
                        if not known(t) or t >= 4:
                            pool.wait_ge(s.heads, t - 3)
                            pool.wait_ge(const_ready, 1)
                        nc.gpsimd.tensor_copy(Vh[:, p, 0:tiles, ds(8 * t - 16, 8)],
                                              zero[:, 0:8 * tiles].rearrange("p (t d) -> p t d", t=tiles)
                                              ).then_inc(s.pool_chain, 1)
                        pool.wait_ge(s.pool_chain, t - 1)
                        pool.wait_ge(const_ready, 1)
                        nc.gpsimd.tensor_copy(Vh[:, p, 0:tiles, ds(8 * t, 8)],
                                              V[:, 0:tiles, ds(8 * t - 16, 8)]).then_inc(s.vh_ready, 1)

                keys(0, 0)
                for t in range(4):
                    step(t, t % 2)
                with pool.Fori(2, H // 2 - 1) as i:
                    step(2 * i, 0)
                    step(2 * i + 1, 1)
                step(H - 2, 0)
                for t in range(H - 1, H + 2):
                    step(t, t % 2, more_keys=False)
                for p in range(2):
                    pool.wait_ge(s.heads, H)
                    nc.gpsimd.tensor_copy(Vh[:, p, 0:tiles, 8 * (H + p):8 * (H + p) + 8],
                                          zero[:, 0:8 * tiles].rearrange("p (t d) -> p t d", t=tiles)
                                          ).then_inc(s.pool_chain, 1)
                pool.wait_ge(s.pool_chain, H + 2)

            root(0)
            root(1)
            masked_heads(a0)
            root(2)
            pool.wait_ge(ln_done, 3 * NT)
            pool.wait_ge(ld.vectors, 48)
            nc.gpsimd.tensor_tensor(XB[:], X[:], row[:, 1, :].unsqueeze(1).broadcast_to([P, NT, P]),
                                    ALU.add).then_inc(x0.base, 1)
            root(3)
            pool.wait_ge(turned, 3)
            nc.gpsimd.memset(QC[1], 0.0).then_inc(pads, 1)

            none = zero[:, 0:P].rearrange("p (h d) -> p h d", h=2).unsqueeze(1).broadcast_to([P, 8, 2, XD])

            def values(c, p):
                pool.wait_ge(x0.v, c + 1)
                nc.gpsimd.tensor_tensor(VC[:, p, :, :, 0, :], VF, none, ALU.add).then_inc(x0.v_high, 1)
                pool.wait_ge(x0.v_high, c + 1)
                nc.gpsimd.tensor_tensor(VC[:, p, :, :, 1, :], VF, VC[:, p, :, :, 0, :], ALU.subtract
                                        ).then_inc(x0.v_parts, 1)

            values(0, 0)
            values(1, 1)
            with pool.Fori(1, XC // 2) as i:
                values(2 * i, 0)
                values(2 * i + 1, 1)
            root(4)
            root(5)
            root(6)
            nc.gpsimd.memset(KT[:].rearrange("p (b k) -> p b k", b=B)[:, :, 0:W], 0.0).then_inc(pads, 1)
            pool.wait_ge(pads, 2)
            pool.wait_ge(ln_done, 7 * NT)
            nc.gpsimd.tensor_tensor(XB[:], X[:], row[:, 2, :].unsqueeze(1).broadcast_to([P, NT, P]),
                                    ALU.add).then_inc(a1.bias_added, 1)
            masked_heads(a1)
            root(7)
            pool.wait_ge(ln_done, 8 * NT)
            nc.gpsimd.tensor_tensor(XB[:], X[:], row[:, 3, :].unsqueeze(1).broadcast_to([P, NT, P]),
                                    ALU.add).then_inc(x1.bias_added, 1)
            masked_heads(x1)
            root(8)
            root(9)

        @block.tensor
        def _(pe):
            def turn(norms, k, bank=Y_BANK):
                for t in range(NT):
                    if norms:
                        pe.wait_ge(ln_done, NT * (norms - 1) + t + 1)
                    last = nc.tensor.transpose(ps[:, bank, t * P:(t + 1) * P], k[:, t, :], ident)
                last.then_inc(turned, 1)

            def head_steps(s):
                window = s.kind == "window"
                qw = W if window else P

                def step(t, p):
                    if not known(t) or t < H:
                        pe.wait_ge(s.kh_ready, t + 1)
                        if not known(t) or t >= 2:
                            pe.wait_ge(s.neg, t - 1)
                        for b in range(B):
                            if window:
                                for c in range(T // W):
                                    last = nc.tensor.matmul(
                                        ps[W * (c % 2):W * (c % 2) + W, 2 * p, ds((2 * b + c // 2) * P, P)],
                                        QT[:, b * T + c * W:b * T + (c + 1) * W],
                                        Kh[:, p, b * PAD + c * W:b * PAD + c * W + 2 * W], start=True, stop=True)
                            else:
                                nc.tensor.matmul(ps[:, 2 * p + b, 0:P], QT[:, b * T:b * T + P],
                                                 Kh[:, p, b * T:b * T + P], start=True, stop=True)
                                last = nc.tensor.matmul(ps[:, 2 * p + b, P:3 * P], QT[:, b * T + P:b * T + T],
                                                        Kh[:, p, b * T:b * T + T], start=True, stop=True)
                        last.then_inc(s.scores, 1)
                    if not known(t) or 2 <= t < H + 2:
                        pe.wait_ge(s.probs, t - 1)
                        if not known(t) or t >= 3:
                            pe.wait_ge(s.flip_act, t - 2)
                            if not window:
                                pe.wait_ge(s.flip_dve, t - 2)
                        if window:
                            for k in range(4):
                                last = nc.tensor.transpose(ps[:, PT_BANK, k * P:(k + 1) * P],
                                                           PR[:, p, k * P:(k + 1) * P], ident)
                        else:
                            for b in range(B):
                                for k in range(3):
                                    last = nc.tensor.transpose(ps[:, PT_BANK + b, k * P:(k + 1) * P],
                                                               PR[:, p, b * BLK + k * P:b * BLK + (k + 1) * P], ident)
                        last.then_inc(s.flipped, 1)
                    if not known(t) or t >= 3:
                        q = 1 - p
                        pe.wait_ge(s.flip_act, t - 2)
                        if not window:
                            pe.wait_ge(s.flip_dve, t - 2)
                        pe.wait_ge(s.vh_ready, t - 2)
                        for b in range(B):
                            if window:
                                for c in range(T // W):
                                    last = nc.tensor.matmul(
                                        ps[:, O_BANK, b * T + c * W:b * T + (c + 1) * W],
                                        Vh[:, q, b * 4 + c, 16:16 + P],
                                        PTS[:, q, (2 * b + c // 2) * P + W * (c % 2):(2 * b + c // 2) * P + W * (c % 2) + W],
                                        start=False, stop=False, skip_group_check=True)
                            else:
                                nc.tensor.matmul(ps[:, O_BANK, b * T:b * T + T], Vh[:, q, 2 * b, 16:16 + P],
                                                 PTS[:, q, b * BLK:b * BLK + T],
                                                 start=False, stop=False, skip_group_check=True)
                                last = nc.tensor.matmul(ps[:, O_BANK, b * T + P:b * T + T], Vh[:, q, 2 * b + 1, 16:16 + P],
                                                        PTS[:, q, b * BLK + T:b * BLK + BLK],
                                                        start=False, stop=False, skip_group_check=True)
                        last.then_inc(s.heads, 1)

                nc.tensor.matmul(ps[:, O_BANK, :], zh[:],
                                 hs[:, G_ONE:G_ONE + 512], start=True, stop=False, skip_group_check=True)
                run_steps(pe, H, step)

            def out_proj(s, w):
                pe.wait_ge(s.act_out, 3)
                for t in range(NT):
                    last = nc.tensor.matmul(ps[:, Y_BANK, t * P:(t + 1) * P], OT[:, t * P:(t + 1) * P], w[:, 3, :],
                                            start=True, stop=True)
                last.then_inc(s.proj, 1)

            pe.wait_ge(ld.lora, 16)
            for k in range(3):
                last = nc.tensor.matmul(ps[:, 0, k * P:(k + 1) * P], lora_sb[:, k, :], lora_sb[:, 3 + k, :],
                                        start=True, stop=True)
            last.then_inc(weff_ps, 1)
            pe.wait_ge(ld.x, 16)
            pe.wait_ge(ld.consts, 16)
            turn(0, X)
            pe.wait_ge(weff, 1)
            pe.wait_ge(turned_out, 1)
            nc.tensor.matmul(ps[:, 1, :], wa0[:, 0, :], XT[:], start=True, stop=True).then_inc(a0.proj, 1)
            nc.tensor.matmul(ps[:, 2, :], wa0[:, 1, :], XT[:], start=True, stop=True).then_inc(a0.proj, 1)
            for t in range(NT):
                last = nc.tensor.matmul(ps[:, 3, t * P:(t + 1) * P], XT[:, t * P:(t + 1) * P], wa0[:, 2, :],
                                        start=True, stop=True)
            last.then_inc(a0.proj, 1)
            pe.wait_ge(a0.act_out, 2)
            pe.wait_ge(a0.k_out, 1)
            pe.wait_ge(ld.halfs, 16)
            pe.wait_ge(const_ready, 1)
            head_steps(a0)
            out_proj(a0, wa0)

            for k, src in enumerate((CN[:, 0:4], CN[:, 4:8], None)):
                if src is not None:
                    turn(k + 1, src, k)
                else:
                    pe.wait_ge(ld.ctx, 16)
                    for t in range(NT):
                        last = nc.tensor.transpose(ps[:, 2, t * P:(t + 1) * P], C[:, 4 * (t // 2) + t % 2, :], ident)
                    last.then_inc(turned, 1)
            pe.wait_ge(x0.null_w, 1)
            pe.wait_ge(ld.wo_all, 32)
            for h in range(H):
                last = nc.tensor.matmul(ps[0:H, 3, 0:P], nv16[:, h, :], wo_all[:, h, :],
                                        start=(h == 0), stop=(h == H - 1))
            for c in range(XC):
                last = nc.tensor.matmul(ps[:, 3, P + 2 * c:P + 2 * c + 2], wqt[:, c, :], nk2[:], start=True, stop=True)
            last.then_inc(x0.nvo_ps, 1)

            def project_q(c, p):
                pe.wait_ge(x0.w_odd if p else x0.w_even, 16 * (c // 2 + 1) if known(c) else (c - p) * 8 + 16)
                nc.tensor.matmul(ps[:, 0, :], x0ring[:, p, 0, :], XT[:], start=True, stop=True).then_inc(x0.q_ps, 1)

            def project_k(c, p):
                for b in range(B):
                    last = nc.tensor.matmul(ps[:, 2 + b, :], x0ring[:, p, 1, :], CNT[:, b * S2:(b + 1) * S2],
                                            start=True, stop=True)
                last.then_inc(x0.k_ps, 1)

            def project_v(c, p):
                for t in range(8):
                    last = nc.tensor.matmul(ps[:, t // 4, (t % 4) * P:(t % 4 + 1) * P], CNT[:, t * P:(t + 1) * P],
                                            x0ring[:, p, 2, :], start=True, stop=True)
                last.then_inc(x0.v_ps, 1)

            def out_chunk(c, p):
                for k in range(2):
                    for t in range(NT):
                        nc.tensor.matmul(ps[:, Y_BANK, t * P:(t + 1) * P], OC[:, p, k, t * P:(t + 1) * P],
                                         wo_all[:, ds(2 * c + k, 1), :].rearrange("p a d -> p (a d)"),
                                         start=False, stop=False, skip_group_check=True)

            def unit(c, cp, j, last_chunk=False):
                u, p = 4 * c + j, j % 2
                if not known(u) or u < 4 * XC:
                    if j == 0:
                        pe.wait_ge(x0.v, c + 1)
                    elif j == 1:
                        if known(c) and c == 0:
                            pe.wait_ge(x0.k, 1)
                        else:
                            pe.wait_ge(x0.neg, 4 * c)
                    elif last_chunk:
                        pe.wait_ge(x0.neg, u - 1)
                    else:
                        pe.wait_ge(x0.k if j == 3 else x0.q, c + 2)
                    b = j // 2
                    for k in range(2):
                        last = nc.tensor.matmul(ps[:, 2 * p + k, :], QC[cp][:, p, b * T + k * P:b * T + (k + 1) * P],
                                                KC[:, cp, b * S2:(b + 1) * S2], start=True, stop=True)
                    last.then_inc(x0.scores, 1)
                    if j == 1 and not last_chunk:
                        pe.wait_ge(x0.neg, 4 * c + 1)
                        project_q(c + 1, 1 - cp)
                    if j == 3 and not last_chunk:
                        pe.wait_ge(x0.neg, 4 * c + 3)
                        project_v(c + 1, 1 - cp)
                if not known(u) or 2 <= u < 4 * XC + 2:
                    for part, (src, ready, used) in enumerate(((PRH, x0.high, x0.flip_act), (PRL, x0.probs, x0.flip_dve))):
                        pe.wait_ge(ready, u - 1)
                        if not known(u) or u >= 3:
                            pe.wait_ge(used, u - 2)
                        for kt in range(4):
                            for k in range(2):
                                last = nc.tensor.transpose(PT16[:, part, kt * T + k * P:kt * T + (k + 1) * P],
                                                           src[:, p, k * S2 + kt * P:k * S2 + (kt + 1) * P], ident16)
                        last.then_inc(x0.flipped, 1)
                if (not known(u) or u >= 3) and (j < 3 or not known(c) or c < XC):
                    vp, w = (cp, 0) if j == 3 else (1 - cp, j + 1)
                    b, h = w // 2, w % 2
                    if not known(u) or u >= 4:
                        pe.wait_ge(x0.oc, u - 3)
                    if j == 3:
                        pe.wait_ge(x0.v_parts, c + 1)
                    for part, (src, ready) in enumerate(((PTH, x0.flip_act), (PTL, x0.flip_dve))):
                        pe.wait_ge(ready, u - 2)
                        for kt in range(4):
                            last = nc.tensor.matmul(ps[:, O_BANK, 0:T],
                                                    VC[:, vp, 4 * b + kt, h].rearrange("p two d -> p (two d)"),
                                                    src[:, 1 - p, kt * T:(kt + 1) * T],
                                                    start=(kt == 0 and part == 0), stop=(kt == 3 and part == 1))
                    last.then_inc(x0.heads, 1)
                if j == 0 and (not known(c) or c >= 2):
                    pe.wait_ge(x0.oc, 4 * c - 4)
                    out_chunk(c - 2, cp)
                if not known(u) or u < 4 * XC:
                    if j == 1 and not last_chunk:
                        pe.wait_ge(x0.neg, 4 * c + 2)
                        project_k(c + 1, 1 - cp)

            pe.wait_ge(a0.resid, 1)
            turn(4, XN)
            pe.wait_ge(turned_out, 5)
            project_q(0, 0)
            project_k(0, 0)
            pe.wait_ge(x0.nvo, 1)
            for t in range(NT):
                last = nc.tensor.matmul(ps[:, Y_BANK, t * H:(t + 1) * H], XT[:, t * P:(t + 1) * P], WN[:],
                                        start=True, stop=True)
            last.then_inc(x0.sn_ps, 1)
            pe.wait_ge(x0.q, 1)
            project_v(0, 0)
            pe.wait_ge(x0.sn, 1)
            nc.tensor.matmul(ps[:, Y_BANK, :], zh[:], hs[:, G_ONE:G_ONE + 512], start=True, stop=False,
                             skip_group_check=True)
            for j in range(8):
                unit(j // 4, j // 4, j % 4)
            with pe.Fori(1, XC // 2 - 1) as i:
                for j in range(8):
                    unit(2 * i + j // 4, j // 4, j % 4)
            for j in range(8):
                unit(XC - 2 + j // 4, j // 4, j % 4, last_chunk=j >= 4)
            for j in range(3):
                unit(XC, 0, j)
            pe.wait_ge(x0.oc, 4 * XC)
            out_chunk(XC - 1, 1)
            pe.wait_ge(x0.probs, 4 * XC)
            for t in range(NT):
                last = nc.tensor.transpose(ps[0:H, 0, t * P:(t + 1) * P], PNN[:, t, :], ident)
            last.then_inc(x0.pnt_ps, 1)
            pe.wait_ge(x0.pnt, 1)
            pe.wait_ge(x0.nvo, 1)
            for t in range(NT):
                last = nc.tensor.matmul(ps[:, Y_BANK, t * P:(t + 1) * P], PNT[:, t * P:(t + 1) * P], nvo[:],
                                        start=False, stop=False, skip_group_check=True)
            last.then_inc(x0.out, 1)

            turn(6, X, 0)
            pe.wait_ge(turned_out, 6)
            pe.wait_ge(ld.gate0, 16)
            for t in range(NT):
                last = nc.tensor.matmul(ps[:, Y_BANK, t * E0:(t + 1) * E0], XT[:, t * P:(t + 1) * P], g0w[:],
                                        start=True, stop=True)
            last.then_inc(e0.logits, 1)
            pe.wait_ge(ld.w_e0, 16)

            def hidden(e):
                for k in range(2):
                    if e >= 2:
                        pe.wait_ge(e0.silu, 2 * (e - 2) + k + 1)
                    nc.tensor.matmul(ps[:, 2 * (e % 2) + k, :], e0w[:, e, 0, k * P:(k + 1) * P], XT[:],
                                     start=True, stop=True).then_inc(e0.hidden, 1)

            hidden(0)
            for e in range(E0):
                if e + 1 < E0:
                    hidden(e + 1)
                pe.wait_ge(e0.silu, 2 * e + 2)
                if e >= 2:
                    pe.wait_ge(e0.acc, e - 1)
                for t in range(NT):
                    for k in range(2):
                        last = nc.tensor.matmul(ps[:, 4 + e % 2, t * P:(t + 1) * P], H0[:, e % 2, k, t * P:(t + 1) * P],
                                                e0w[:, e, 1, k * P:(k + 1) * P], start=(k == 0), stop=(k == 1))
                last.then_inc(e0.y, 1)

            turn(7, X)
            pe.wait_ge(turned_out, 7)
            pe.wait_ge(ld.w_a1, 16)
            nc.tensor.matmul(ps[:, 0, :].rearrange("p (b t) -> p b t", b=B), wa1[:, 0, :], XTP[:, :, W:],
                             start=True, stop=True).then_inc(a1.proj, 1)
            nc.tensor.matmul(ps[:, 1, :].rearrange("p (b t) -> p b t", b=B), wa1[:, 1, :], XTP[:, :, W:],
                             start=True, stop=True).then_inc(a1.proj, 1)
            for b in range(B):
                for c in range(T // W):
                    last = nc.tensor.matmul(ps[:, 2 + b, c * P:(c + 1) * P], XTP[:, b, c * W:c * W + 2 * W],
                                            wa1[:, 2, :], start=True, stop=True)
            last.then_inc(a1.proj, 1)
            pe.wait_ge(a1.act_out, 2)
            pe.wait_ge(a1.k_out, 1)
            head_steps(a1)
            out_proj(a1, wa1)

            pe.wait_ge(ld.late, 80)
            nc.tensor.matmul(ps[:, 1, :], wx1[:, 1, :], CT[:], start=True, stop=True).then_inc(x1.proj, 1)
            for t in range(NT):
                last = nc.tensor.matmul(ps[:, 2, t * P:(t + 1) * P], CT[:, t * P:(t + 1) * P], wx1[:, 2, :],
                                        start=True, stop=True)
            last.then_inc(x1.proj, 1)
            for b in range(B):
                for t in range(4):
                    last = nc.tensor.matmul(ps[:, 3, b:b + 1], C[:, 4 * b + t, :], mean_col[:],
                                            start=(t == 0), stop=(t == 3))
            last.then_inc(x1m.mean_ps, 1)
            pe.wait_ge(x1m.mean, 1)
            nc.tensor.matmul(ps[:, 4, 0:B], wx1[:, 2, :], MC[:], start=True, stop=True).then_inc(x1m.value_ps, 1)
            turn(8, X)
            pe.wait_ge(turned_out, 8)
            nc.tensor.matmul(ps[:, 0, :], wx1[:, 0, :], XT[:], start=True, stop=True).then_inc(x1.proj, 1)
            pe.wait_ge(x1.act_out, 2)
            pe.wait_ge(x1.k_out, 1)
            pe.wait_ge(x1m.value, 1)
            head_steps(x1)
            pe.wait_ge(x1m.patched, 1)
            out_proj(x1, wx1)

            turn(9, X)
            pe.wait_ge(turned_out, 9)
            pe.wait_ge(ld.late, 80)
            for t in range(NT):
                last = nc.tensor.matmul(ps[:, 4, t * E1:(t + 1) * E1], XT[:, t * P:(t + 1) * P], g1w[:],
                                        start=True, stop=True)
            last.then_inc(e1.logits, 1)
            pe.wait_ge(ld.late, 80)
            for k in range(4):
                last = nc.tensor.matmul(ps[0:F1, k, :], ws13_sb[:, k, :], XT[:], start=True, stop=True)
            last.then_inc(e1.zh_ps, 1)
            pe.wait_ge(e1.sel, SEL_DONE)
            for t in range(NT):
                for j in range(t + 1):
                    g = G_CUM if j == t else G_ONE
                    last = nc.tensor.matmul(ps[:, 5, t * E1:(t + 1) * E1], hs[:, g:g + P], SELh[:, j, :],
                                            start=(j == 0), stop=(j == t))
            last.then_inc(e1.count_ps, 1)
            pe.wait_ge(e1.z_mult, 1)
            for t in range(NT):
                for k in range(2):
                    nc.tensor.matmul(ps[:, O_BANK, t * P:(t + 1) * P], ZH[:, k, t * P:(t + 1) * P], ws2_sb[:, k, :],
                                     start=(t == 0 and k == 0), stop=False, skip_group_check=True)
            pe.wait_ge(e1.parts, 2)
            for g in range(8):
                for t in range(NT):
                    if t == 0:
                        pe.wait_ge(e1.onehot, g + 1)
                    if t == 0 and g >= 4:
                        pe.wait_ge(e1.gather_act, g - 3)
                    for part in (XH, XL):
                        last = nc.tensor.matmul(ps[:, g % 4, :], part[:, t, :],
                                                PH[:, t, 8 * g:8 * g + 8, :].rearrange("p s e -> p (s e)"),
                                                start=(t == 0 and part is XH), stop=(t == NT - 1 and part is XL))
                last.then_inc(e1.gather_ps, 1)
            pe.wait_ge(e1.gather_act, 8)
            ring_full = (e1.w0, e1.w1, e1.w2, e1.w3)

            def pair(t, r):
                p = r % 2
                if not known(t) or t < PAIRS:
                    pe.wait_ge(e1.pw, t + 1)
                    if not known(t) or t >= 2:
                        pe.wait_ge(e1.pm, t - 1)
                    for k in range(NT):
                        last = nc.tensor.transpose(ps[:, p, k * P:(k + 1) * P], PW[:, p, k, :], ident)
                    last.then_inc(e1.pw_t, 1)
                    if not known(t) or t >= 2:
                        pe.wait_ge(e1.hg, t - 1)
                    pe.wait_ge(ring_full[r], ((t - r) * (32 // RING) + 32) if not known(t) else 32 * (t // RING + 1))
                    for k in range(4):
                        last = nc.tensor.matmul(ps[0:F1, 2 + p, k * CAP:(k + 1) * CAP], w13r[:, r, 2 * (k % 2) + k // 2, :],
                                                XBT[:, ds(2 * t + k % 2, 1), :].rearrange("p e s -> p (e s)"),
                                                start=True, stop=True)
                    last.then_inc(e1.hidden, 1)
                if not known(t) or 1 <= t < PAIRS + 1:
                    q, rr = 1 - p, (r - 1) % RING
                    pe.wait_ge(e1.hg, t)
                    if not known(t) or t >= 3:
                        pe.wait_ge(e1.ys, t - 2)
                    for k in range(2):
                        last = nc.tensor.matmul(ps[k * CAP:(k + 1) * CAP, 4 + q, 0:P], HG[:, q, k * CAP:(k + 1) * CAP],
                                                w2r[:, rr, k, :], start=True, stop=True)
                    last.then_inc(e1.y, 1)
                if not known(t) or t >= 2:
                    pe.wait_ge(e1.ys, t - 1)
                    for k in range(NT):
                        last = nc.tensor.matmul(ps[:, O_BANK, k * P:(k + 1) * P], PM[:, (r - 2) % RING, k * P:(k + 1) * P], YS[:, p, :],
                                                start=False, stop=False, skip_group_check=True)
                    last.then_inc(e1.added, 1)

            run_pairs(pe, pair)

        @block.scalar
        def _(act):
            act.dma_start(C[:], ctx.rearrange("(t p) d -> p t d", p=P)).then_inc(ld.ctx, 16)
            nc.scalar.preload_act_table(ACT.Exp)

            def head_steps(s):
                window = s.kind == "window"
                peak = s.peak if s.kind == "padded" else s.neg

                def positions(t, p):
                    nc.scalar.mul(negrel[:, p, :], cs[:, C_REL:C_REL + BLK], cs[:, ds(t + C_SL, 1)]).then_inc(s.rel, 1)

                if s.kind == "causal":
                    positions(0, 0)
                    positions(1, 1)

                def step(t, p):
                    if not known(t) or 2 <= t < H + 2:
                        act.wait_ge(s.flipped, t - 1)
                        if not known(t) or t >= 4:
                            act.wait_ge(s.heads, t - 3)
                        w = 512 if window else BLK
                        nc.scalar.copy(PTS[:, p, 0:w], ps[:, PT_BANK, 0:w]).then_inc(s.flip_act, 1)
                    if not known(t) or t < H:
                        act.wait_ge(peak, t + 1)
                        if not known(t) or t >= 2:
                            act.wait_ge(s.flipped, t - 1)
                        if window:
                            parts = [(k * P, P, k) for k in range(4)]
                        else:
                            parts = [(b * BLK + a, w, 2 * b + k) for b in range(B)
                                     for k, (a, w) in enumerate(((0, P), (P, 2 * P)))]
                        for a, w, k in parts:
                            last = nc.scalar.activation(PR[:, p, a:a + w], NS[:, p, a:a + w], ACT.Exp,
                                                        bias=NM[:, p, k:k + 1], scale=-1.0,
                                                        accum_out=RS[:, p, k:k + 1])
                        last.then_inc(s.exps, 1)
                        if s.kind == "causal" and (not known(t) or t < H - 2):
                            positions(t + 2, p)

                run_steps(act, H, step)

            def heads_out(s, bias):
                act.wait_ge(s.heads, H)
                nc.scalar.activation(OT[:], ps[:, O_BANK, :], ACT.Identity, bias=bias).then_inc(s.act_out, 1)

            act.wait_ge(turned, 1)
            nc.scalar.copy(XT[:], ps[:, Y_BANK, :]).then_inc(turned_out, 1)
            act.wait_ge(a0.proj, 1)
            nc.scalar.mul(QT[:], ps[:, 1, :], -DH ** -0.5).then_inc(a0.act_out, 1)
            act.wait_ge(a0.proj, 3)
            nc.scalar.copy(V[:, 0:NT, :], ps[:, 3, :].rearrange("p (t d) -> p t d", t=NT)).then_inc(a0.act_out, 1)
            head_steps(a0)
            act.wait_ge(const_ready, 1)
            heads_out(a0, zcol[:])

            act.wait_ge(ld.vectors, 48)
            for k in range(2):
                act.wait_ge(turned, k + 2)
                nc.scalar.activation(CNT[:, k * S2:(k + 1) * S2], ps[:, k, :], ACT.Identity, bias=vec[:, 3:4],
                                     scale=vec[:, 2:3]).then_inc(turned_out, 1)
            act.wait_ge(turned, 4)
            nc.scalar.copy(CT[:], ps[:, 2, :]).then_inc(turned_out, 1)
            act.wait_ge(x0.nvo_ps, 1)
            nc.scalar.copy(nvo[:], ps[0:H, 3, 0:P])
            nc.scalar.copy(WN[:], ps[:, 3, P:P + H]).then_inc(x0.nvo, 1)
            act.wait_ge(turned, 5)
            nc.scalar.activation(XT[:], ps[:, Y_BANK, :], ACT.Identity, bias=vec[:, 1:2],
                                 scale=vec[:, 0:1]).then_inc(turned_out, 1)

            def q_out(c, p):
                act.wait_ge(x0.q_ps, c + 1)
                for k in range(2):
                    r = XD * k
                    last = nc.scalar.mul(QC[p][r:r + XD, k, :], ps[r:r + XD, 0, :], -H ** -0.5)
                last.then_inc(x0.q, 1)

            def k_out(c, p):
                act.wait_ge(x0.k_ps, c + 1)
                nc.scalar.copy(KC[:, p, :].rearrange("p (b k) -> p b k", b=B), ps[:, 2:4, :]).then_inc(x0.k, 1)

            def v_out(c, p):
                act.wait_ge(x0.v_ps, c + 1)
                if not known(c) or c:
                    act.wait_ge(x0.v_parts, c)
                nc.scalar.mul(VF.rearrange("p (b t) h d -> p b (t h d)", b=2), ps[:, 0:2, :], V_UP).then_inc(x0.v, 1)

            def unit(c, cp, j, last_chunk=False):
                u, p = 4 * c + j, j % 2
                if not known(u) or u >= 4:
                    act.wait_ge(x0.heads, u - 3)
                    nc.scalar.mul(OC[:, 1 - cp, p, (j // 2) * T:(j // 2 + 1) * T],
                                  ps[:, O_BANK, 0:T], 1 / (V_UP * PR_UP)).then_inc(x0.oc, 1)
                if (not known(u) or u < 4 * XC) and not last_chunk:
                    if j == 1:
                        q_out(c + 1, 1 - cp)
                    if j == 3:
                        v_out(c + 1, 1 - cp)
                if not known(u) or 2 <= u < 4 * XC + 2:
                    act.wait_ge(x0.flipped, 2 * u - 3)
                    if not known(u) or u >= 4:
                        act.wait_ge(x0.heads, u - 3)
                    nc.scalar.copy(PTH[:, p, :], PT16[:, 0, :]).then_inc(x0.flip_act, 1)
                if not known(u) or u < 4 * XC:
                    act.wait_ge(x0.peak, u + 1)
                    if not known(u) or u >= 2:
                        act.wait_ge(x0.probs, u - 1)
                    for k in range(2):
                        nc.scalar.activation(PR[:, p, k * S2:(k + 1) * S2], NS[:, p, k * S2:(k + 1) * S2], ACT.Exp,
                                             bias=NM[:, p, k:k + 1], scale=-1.0, accum_out=RS[:, p, k:k + 1])
                    nc.scalar.activation(PN[:, p, :], DN[:, p, :], ACT.Exp).then_inc(x0.exps, 1)
                if (not known(u) or u < 4 * XC) and not last_chunk and j == 1:
                    k_out(c + 1, 1 - cp)

            q_out(0, 0)
            k_out(0, 0)
            v_out(0, 0)
            act.wait_ge(pads, 1)
            for j in range(8):
                unit(j // 4, j // 4, j % 4)
            with act.Fori(1, XC // 2 - 1) as i:
                for j in range(8):
                    unit(2 * i + j // 4, j // 4, j % 4)
            for j in range(8):
                unit(XC - 2 + j // 4, j // 4, j % 4, last_chunk=j >= 4)
            for j in range(4):
                unit(XC, 0, j)
            act.wait_ge(x0.pnt_ps, 1)
            nc.scalar.mul(PNT[:], ps[0:H, 0, :], 1 / PR_UP).then_inc(x0.pnt, 1)

            act.wait_ge(turned, 6)
            nc.scalar.copy(XT[:], ps[:, 0, :]).then_inc(turned_out, 1)
            act.wait_ge(e0.route, 1)
            nc.scalar.activation(EZ0[:], Z0[:], ACT.Exp, scale=-1.0).then_inc(e0.ez, 1)
            for e in range(E0):
                for k in range(2):
                    act.wait_ge(e0.hidden, 2 * e + k + 1)
                    if e >= 2:
                        act.wait_ge(e0.y, e - 1)
                    nc.scalar.activation(H0[:, e % 2, k, :], ps[:, 2 * (e % 2) + k, :], ACT.Silu).then_inc(e0.silu, 1)

            nc.scalar.preload_act_table(ACT.Exp)

            act.wait_ge(turned, 7)
            nc.scalar.copy(XTP[:, :, W:], ps[:, Y_BANK, :].rearrange("p (b t) -> p b t", b=B)).then_inc(turned_out, 1)
            act.wait_ge(a1.proj, 1)
            act.wait_ge(x1m.bq, 1)
            nc.scalar.activation(QT[:], ps[:, 0, :], ACT.Identity, bias=scaled_bq[:, 0:1],
                                 scale=-DH ** -0.5).then_inc(a1.act_out, 1)
            act.wait_ge(a1.proj, 3)
            nc.scalar.copy(V[:].rearrange("p (b t) d -> p b (t d)", b=2), ps[:, 2:4, :]).then_inc(a1.act_out, 1)
            head_steps(a1)
            heads_out(a1, vec[:, 6:7])

            act.wait_ge(x1.proj, 2)
            nc.scalar.copy(V[:, 0:NT, :], ps[:, 2, :].rearrange("p (t d) -> p t d", t=NT)).then_inc(x1.act_out, 1)
            act.wait_ge(x1m.mean_ps, 1)
            nc.scalar.copy(MC[:], ps[:, 3, 0:B]).then_inc(x1m.mean, 1)
            act.wait_ge(x1m.value_ps, 1)
            nc.scalar.activation(MVB[:], ps[:, 4, 0:B], ACT.Identity, bias=vec[:, 9:10]).then_inc(x1m.value, 1)
            act.wait_ge(turned, 8)
            nc.scalar.copy(XT[:], ps[:, Y_BANK, :]).then_inc(turned_out, 1)
            act.wait_ge(x1.proj, 3)
            nc.scalar.activation(QT[:], ps[:, 0, :], ACT.Identity, bias=scaled_bq[:, 1:2],
                                 scale=-DH ** -0.5).then_inc(x1.act_out, 1)
            head_steps(x1)
            heads_out(x1, vec[:, 9:10])

            act.wait_ge(turned, 9)
            nc.scalar.copy(XT[:], ps[:, Y_BANK, :]).then_inc(turned_out, 1)
            act.wait_ge(e1.low, 1)
            for t in range(NT):
                last = nc.scalar.activation(EX[:, t, :], ps[:, 4, t * E1:(t + 1) * E1], ACT.Exp, bias=NMX[:, t:t + 1],
                                            accum_out=SX[:, t:t + 1])
            last.then_inc(e1.ex, 1)
            act.wait_ge(e1.zh_ps, 1)
            nc.scalar.activation(ZG[:], ps[0:F1, 0:2, :], ACT.Silu).then_inc(e1.z_silu, 1)
            for g in range(8):
                act.wait_ge(e1.gather_ps, g + 1)
                nc.scalar.copy(XBT[:, :, 8 * g:8 * g + 8].rearrange("p e s -> p s e"),
                               ps[:, g % 4, :].rearrange("p (s e) -> p s e", s=8)).then_inc(e1.gather_act, 1)

            def pair(t, r):
                p = r % 2
                if not known(t) or t < PAIRS:
                    act.wait_ge(e1.pw_t, t + 1)
                    if not known(t) or t >= 4:
                        act.wait_ge(e1.added, t - 3)
                    nc.scalar.copy(PM[:, r, :], ps[:, p, :]).then_inc(e1.pm, 1)
                    act.wait_ge(e1.hidden, t + 1)
                    if not known(t) or t >= 2:
                        act.wait_ge(e1.hg, t - 1)
                    nc.scalar.activation(GG[:, p, :], ps[0:F1, 2 + p, 0:2 * CAP], ACT.Silu).then_inc(e1.silu, 1)
                if not known(t) or 1 <= t < PAIRS + 1:
                    q = 1 - p
                    act.wait_ge(e1.y, t)
                    if not known(t) or t >= 3:
                        act.wait_ge(e1.added, t - 2)
                    nc.scalar.copy(YS[:, q, :], ps[:, 4 + q, 0:P]).then_inc(e1.ys, 1)

            run_pairs(act, pair)

        @block.vector
        def _(dve):
            def norm(n, src, dst, eps):
                if n:
                    dve.wait_ge(ln_done, n * NT)
                for t in range(NT):
                    last = nc.vector.bn_stats(st[:, t, :], src[:, t, :])
                last.then_inc(ln_chain, 1)
                dve.wait_ge(ln_chain, 2 * n + 1)
                for t in range(NT):
                    last = nc.vector.bn_aggr(mv[:, t, :], st[:, t, :])
                last.then_inc(ln_chain, 1)
                dve.wait_ge(ln_chain, 2 * n + 2)
                nc.vector.tensor_scalar(ve[:], mv[:, :, 1], eps, None, ALU.add).then_inc(ln_var, 1)
                dve.wait_ge(ln_rstd, n + 1)
                for t in range(NT):
                    nc.vector.tensor_scalar(dst[:, t, :], src[:, t, :], mv[:, t, 0:1], rstd[:, t:t + 1],
                                            ALU.subtract, ALU.mult).then_inc(ln_done, 1)

            def head_steps(s):
                window = s.kind == "window"

                def step(t, p):
                    if not known(t) or t < H:
                        dve.wait_ge(s.scores, t + 1)
                        if s.kind == "causal":
                            dve.wait_ge(s.rel, t + 1)
                        nc.vector.memset(gate[:, p:p + 1], 0.0)
                        if window:
                            for k in range(4):
                                last = nc.vector.tensor_tensor_reduce(
                                    out=NS[:, p, k * P:(k + 1) * P], in0=ps[:, 2 * p, k * P:(k + 1) * P],
                                    in1=cs[:, C_WIN + k * P:C_WIN + (k + 1) * P], scale=1.0, scalar=3e38,
                                    op0=ALU.add, op1=ALU.min, accum_out=NM[:, p, k:k + 1])
                            last.then_inc(s.neg, 1)
                        else:
                            to = MN if s.kind == "padded" else NM
                            for b in range(B):
                                terms = negrel[:, b if s.kind == "padded" else p, :]
                                for k, (a, w) in enumerate(((0, P), (P, 2 * P))):
                                    last = nc.vector.tensor_tensor_reduce(
                                        out=NS[:, p, b * BLK + a:b * BLK + a + w], in0=ps[:, 2 * p + b, a:a + w],
                                        in1=terms[:, a:a + w], scale=1.0, scalar=3e38, op0=ALU.add, op1=ALU.min,
                                        accum_out=to[:, p, 2 * b + k:2 * b + k + 1])
                            last.then_inc(s.neg, 1)
                        if s.kind == "padded":
                            dve.wait_ge(s.neg, t + 1)
                            nc.vector.tensor_scalar(NM[:, p, :], MN[:, p, :], peak_limit[:], None, ALU.min).then_inc(s.peak, 1)
                    if not known(t) or 1 <= t < H + 1:
                        q = 1 - p
                        dve.wait_ge(s.exps, t)
                        nc.vector.reciprocal(RI[:, q, :], RS[:, q, :]).then_inc(s.norm_chain, 1)
                        dve.wait_ge(s.norm_chain, t)
                        if window:
                            parts = [(k * P, P, k) for k in range(4)]
                        else:
                            parts = [(b * BLK + a, w, 2 * b + k) for b in range(B)
                                     for k, (a, w) in enumerate(((0, P), (P, 2 * P)))]
                        for a, w, k in parts:
                            last = nc.vector.tensor_scalar(PR[:, q, a:a + w], PR[:, q, a:a + w], RI[:, q, k:k + 1],
                                                           None, ALU.mult)
                        last.then_inc(s.probs, 1)
                    if (not known(t) or 2 <= t < H + 2) and not window:
                        dve.wait_ge(s.flipped, t - 1)
                        if not known(t) or t >= 4:
                            dve.wait_ge(s.heads, t - 3)
                        nc.vector.tensor_copy(PTS[:, p, BLK:2 * BLK], ps[:, PT_BANK + 1, 0:BLK]).then_inc(s.flip_dve, 1)

                run_steps(dve, H, step)

            dve.wait_ge(weff_ps, 1)
            dve.wait_ge(ld.w_a0, 16)
            nc.vector.scalar_tensor_tensor(wa0[:, 0:3, :], ps[:, 0, 0:3 * P].rearrange("p (k d) -> p k d", k=3), 2.0,
                                           wa0[:, 0:3, :], ALU.mult, ALU.add).then_inc(weff, 1)
            dve.wait_ge(ld.ctx, 16)
            norm(0, C[:, 0:4], CN[:, 0:4], EPS_X)
            dve.wait_ge(a0.proj, 2)
            nc.vector.tensor_copy(KT[:, 0:N], ps[:, 2, :]).then_inc(a0.k_out, 1)
            norm(1, C[:, 4:8], CN[:, 4:8], EPS_X)
            dve.wait_ge(ld.nkv, 16)
            dve.wait_ge(ld.more_consts, 16)
            nc.vector.tensor_scalar(nk2[:], cs[:, C_HALF:C_HALF + 2], nkv[:, 0:1], None, ALU.mult)
            nc.vector.tensor_scalar(nv16[:].rearrange("p c h -> p (c h)"), cs[:, C_NH:C_NH + H * H], nkv[:, 1:2], None,
                                    ALU.mult).then_inc(x0.null_w, 1)
            dve.wait_ge(ld.mask, 32)
            nc.vector.tensor_scalar(negpad[:], maskb[:, 0], -BIG, BIG, ALU.mult, ALU.add).then_inc(x0.negpad, 1)
            head_steps(a0)
            dve.wait_ge(a0.proj, 4)
            nc.vector.tensor_tensor(R[:], ps[:, Y_BANK, :].rearrange("p (t d) -> p t d", t=NT), X[:],
                                    ALU.add).then_inc(a0.resid, 1)
            dve.wait_ge(a0.resid, 1)
            norm(2, R, X, EPS_POST)

            dve.wait_ge(ln_done, 3 * NT)
            norm(3, X, XN, EPS_X)
            dve.wait_ge(x0.negpad, 1)

            def unit(c, cp, j, last_chunk=False):
                u, p = 4 * c + j, j % 2
                b = j // 2
                if not known(u) or 1 <= u < 4 * XC + 1:
                    q = 1 - p
                    pb, pc = ((j - 1) // 2, c) if j else (1, c - 1)
                    dve.wait_ge(x0.exps, u)
                    for k in range(2):
                        last = nc.vector.tensor_scalar(TS[:, q, k:k + 1], RS[:, q, k:k + 1], PN[:, q, k:k + 1], 1 / PR_UP,
                                                       ALU.add, ALU.mult)
                    last.then_inc(x0.sums, 1)
                    dve.wait_ge(x0.sums, 2 * u - 1)
                    nc.vector.reciprocal(RI[:, q, 0:2], TS[:, q, :]).then_inc(x0.sums, 1)
                    dve.wait_ge(x0.sums, 2 * u)
                    for k in range(2):
                        last = nc.vector.tensor_scalar(PRH[:, q, k * S2:(k + 1) * S2], PR[:, q, k * S2:(k + 1) * S2],
                                                       RI[:, q, k:k + 1], None, ALU.mult)
                    last.then_inc(x0.high, 1)
                if not known(u) or u < 4 * XC:
                    dve.wait_ge(x0.scores, u + 1)
                    ns = NS[:, p, :].rearrange("p (k s) -> p k s", k=2)
                    null = SN[:, 2 * b:2 * b + 2, ds(2 * c + p, 1)]
                    nc.vector.tensor_scalar(NM[:, p, 0:2].unsqueeze(2), null, 1.0, None, ALU.mult)
                    for k in range(2):
                        last = nc.vector.tensor_tensor_reduce(out=ns[:, k, :], in0=ps[:, 2 * p + k, :],
                                                              in1=negpad[:, b, :], scale=1.0, scalar=3e38,
                                                              op0=ALU.add, op1=ALU.min, accum_out=MN[:, p, k:k + 1])
                    last.then_inc(x0.neg, 1)
                    dve.wait_ge(x0.neg, u + 1)
                    nc.vector.tensor_tensor(NM[:, p, 0:2], MN[:, p, 0:2], NM[:, p, 0:2], ALU.min).then_inc(x0.low, 1)
                    dve.wait_ge(x0.low, u + 1)
                    nc.vector.tensor_tensor(DN[:, p, :].unsqueeze(2), NM[:, p, 0:2].unsqueeze(2), null, ALU.subtract).then_inc(x0.peak, 1)
                if not known(u) or 1 <= u < 4 * XC + 1:
                    nc.vector.tensor_tensor(PNN[:, 2 * pb:2 * pb + 2, ds(2 * pc + q, 1)], PN[:, q, :].unsqueeze(2),
                                            RI[:, q, 0:2].unsqueeze(2), ALU.mult)
                    dve.wait_ge(x0.high, u)
                    for k in range(2):
                        last = nc.vector.scalar_tensor_tensor(PRL[:, q, k * S2:(k + 1) * S2], PR[:, q, k * S2:(k + 1) * S2],
                                                              RI[:, q, k:k + 1], PRH[:, q, k * S2:(k + 1) * S2],
                                                              ALU.mult, ALU.subtract)
                    last.then_inc(x0.probs, 1)
                if not known(u) or 2 <= u < 4 * XC + 2:
                    dve.wait_ge(x0.flipped, 2 * u - 2)
                    if not known(u) or u >= 4:
                        dve.wait_ge(x0.heads, u - 3)
                    nc.vector.tensor_copy(PTL[:, p, :], PT16[:, 1, :]).then_inc(x0.flip_dve, 1)

            dve.wait_ge(x0.sn_ps, 1)
            nc.vector.tensor_scalar(SN[:], ps[:, Y_BANK, 0:NT * H].rearrange("p (t h) -> p t h", t=NT), -H ** -0.5, None,
                                    ALU.mult).then_inc(x0.sn, 1)
            for j in range(8):
                unit(j // 4, j // 4, j % 4)
            with dve.Fori(1, XC // 2 - 1) as i:
                for j in range(8):
                    unit(2 * i + j // 4, j // 4, j % 4)
            for j in range(8):
                unit(XC - 2 + j // 4, j // 4, j % 4, last_chunk=j >= 4)
            for j in range(2):
                unit(XC, 0, j)
            dve.wait_ge(x0.out, 1)
            norm(4, ps[:, Y_BANK, :].rearrange("p (t d) -> p t d", t=NT), XN, EPS_X)
            dve.wait_ge(ln_done, 5 * NT)
            dve.wait_ge(ld.vectors, 48)
            nc.vector.tensor_tensor(R[:], XN[:], row[:, 0, :].unsqueeze(1).broadcast_to([P, NT, P]),
                                    ALU.mult).then_inc(x0.affine, 1)
            dve.wait_ge(x0.affine, 1)
            dve.wait_ge(x0.base, 1)
            nc.vector.tensor_tensor(R[:], R[:], XB[:], ALU.add).then_inc(x0.affine, 1)
            dve.wait_ge(x0.affine, 2)
            norm(5, R, X, EPS_POST)

            chained = [0]

            def then(ins):
                chained[0] += 1
                ins.then_inc(e0.comb, 1)
                dve.wait_ge(e0.comb, chained[0])

            def by_expert(a):
                return a.unsqueeze(3).broadcast_to([P, NT, E0, E0])

            def by_rival(a):
                return a.unsqueeze(2).broadcast_to([P, NT, E0, E0])

            dve.wait_ge(e0.logits, 1)
            dve.wait_ge(ld.vectors, 48)
            nc.vector.tensor_tensor(Z0[:], ps[:, Y_BANK, 0:NT * E0].rearrange("p (t e) -> p t e", t=NT),
                                    grow[:, 0:E0].unsqueeze(1).broadcast_to([P, NT, E0]), ALU.add
                                    ).then_inc(e0.route, 1)
            dve.wait_ge(e0.ez, 1)
            then(nc.vector.tensor_scalar(EZ0[:], EZ0[:], 1.0, None, ALU.add))
            then(nc.vector.reciprocal(GS0[:], EZ0[:]))
            nc.vector.tensor_tensor(GT0[:], by_rival(GS0[:]), by_expert(GS0[:]), ALU.is_gt)
            then(nc.vector.tensor_tensor(EQ0[:], by_rival(GS0[:]), by_expert(GS0[:]), ALU.is_equal))
            then(nc.vector.tensor_tensor(EQ0[:].rearrange("p t a b -> p t (a b)"), EQ0[:].rearrange("p t a b -> p t (a b)"),
                                         cs[:, C_LT:C_ALL].unsqueeze(1).broadcast_to([P, NT, E0 * E0]), ALU.mult))
            then(nc.vector.tensor_tensor(GT0[:], GT0[:], EQ0[:], ALU.add))
            then(nc.vector.tensor_reduce(RK0[:], GT0[:], AX, ALU.add))
            then(nc.vector.scalar_tensor_tensor(SG0[:], RK0[:], K0 - 0.5, GS0[:], ALU.is_lt, ALU.mult))
            then(nc.vector.tensor_reduce(SM0[:], SG0[:], AX, ALU.add))
            then(nc.vector.tensor_scalar(SM0[:], SM0[:], 1e-6, None, ALU.add))
            then(nc.vector.reciprocal(IV0[:], SM0[:]))
            then(nc.vector.tensor_tensor(comb0[:], SG0[:], IV0[:].unsqueeze(2).broadcast_to([P, NT, E0]), ALU.mult))
            for e in range(E0):
                dve.wait_ge(e0.y, e + 1)
                if e:
                    dve.wait_ge(e0.acc, e)
                for t in range(NT):
                    last = nc.vector.scalar_tensor_tensor(R[:, t, :], ps[:, 4 + e % 2, t * P:(t + 1) * P],
                                                          comb0[:, t, e:e + 1], (R if e else X)[:, t, :],
                                                          ALU.mult, ALU.add)
                last.then_inc(e0.acc, 1)
            dve.wait_ge(e0.acc, E0)
            norm(6, R, X, EPS_POST)

            dve.wait_ge(ld.vectors, 48)
            nc.vector.tensor_scalar(scaled_bq[:, 0:1], vec[:, 4:5], -DH ** -0.5, None, ALU.mult)
            nc.vector.tensor_scalar(scaled_bq[:, 1:2], vec[:, 7:8], -DH ** -0.5, None, ALU.mult).then_inc(x1m.bq, 1)
            dve.wait_ge(pads, 2)
            dve.wait_ge(a1.proj, 2)
            nc.vector.tensor_scalar(KT[:].rearrange("p (b k) -> p b k", b=B)[:, :, W:],
                                    ps[:, 1, :].rearrange("p (b t) -> p b t", b=B), vec[:, 5:6], None,
                                    ALU.add).then_inc(a1.k_out, 1)
            head_steps(a1)
            dve.wait_ge(a1.proj, 4)
            dve.wait_ge(a1.bias_added, 1)
            nc.vector.tensor_tensor(R[:], ps[:, Y_BANK, :].rearrange("p (t d) -> p t d", t=NT), XB[:],
                                    ALU.add).then_inc(a1.resid, 1)
            dve.wait_ge(a1.resid, 1)
            norm(7, R, X, EPS_POST)

            shown = maskb[:, 1, :, 0:T]
            nc.vector.tensor_reduce(all_out[:], shown, mybir.AxisListType.XY, ALU.min).then_inc(x1m.flag, 1)
            dve.wait_ge(x1m.flag, 1)
            nc.vector.tensor_scalar(peak_limit[:], all_out[:], BIG * 1e6, 1e20, ALU.mult, ALU.add).then_inc(x1m.flag, 1)
            nc.vector.tensor_scalar(negrel[:], cs[:, C_REL:C_REL + BLK].unsqueeze(1).broadcast_to([P, B, BLK]),
                                    -1e20, BIG, ALU.is_le, ALU.mult).then_inc(x1m.rel, 1)
            dve.wait_ge(x1m.rel, 1)
            nc.vector.scalar_tensor_tensor(negrel[:, :, 0:P], shown[:, :, 0:P], BIG, negrel[:, :, 0:P],
                                           ALU.mult, ALU.add)
            nc.vector.scalar_tensor_tensor(negrel[:, :, P:BLK], shown, BIG, negrel[:, :, P:BLK],
                                           ALU.mult, ALU.add).then_inc(x1m.rel, 1)
            dve.wait_ge(x1.proj, 1)
            nc.vector.tensor_scalar(KT[:, 0:N], ps[:, 1, :], vec[:, 8:9], None, ALU.add).then_inc(x1.k_out, 1)
            dve.wait_ge(x1m.rel, 2)
            dve.wait_ge(x1m.flag, 2)
            head_steps(x1)
            dve.wait_ge(x1.act_out, 3)
            dve.wait_ge(x1m.flag, 1)
            nc.vector.copy_predicated(OT[:].rearrange("p (b t) -> p b t", b=B),
                                      all_out[:].bitcast(mybir.dt.uint32).unsqueeze(2).broadcast_to([P, B, T]),
                                      MVB[:].unsqueeze(2).broadcast_to([P, B, T])).then_inc(x1m.patched, 1)
            dve.wait_ge(x1.proj, 4)
            dve.wait_ge(x1.bias_added, 1)
            nc.vector.tensor_tensor(R[:], ps[:, Y_BANK, :].rearrange("p (t d) -> p t d", t=NT), XB[:],
                                    ALU.add).then_inc(x1.resid, 1)
            dve.wait_ge(x1.resid, 1)
            norm(8, R, X, EPS_POST)

            def each(a):
                return a.unsqueeze(2).broadcast_to([P, NT, E1])

            chosen = [0]

            def then1(ins):
                chosen[0] += 1
                ins.then_inc(e1.sel, 1)
                dve.wait_ge(e1.sel, chosen[0])

            dve.wait_ge(e1.logits, 1)
            then1(nc.vector.tensor_reduce(MX[:], ps[:, 4, 0:NT * E1].rearrange("p (t e) -> p t e", t=NT), AX, ALU.max))
            nc.vector.tensor_scalar(NMX[:], MX[:], -1.0, None, ALU.mult).then_inc(e1.low, 1)
            dve.wait_ge(ln_done, 9 * NT)
            nc.vector.tensor_copy(XH[:], X[:]).then_inc(e1.parts, 1)
            dve.wait_ge(e1.parts, 1)
            nc.vector.tensor_tensor(XL[:], X[:], XH[:], ALU.subtract).then_inc(e1.parts, 1)
            dve.wait_ge(e1.ex, 1)
            then1(nc.vector.reciprocal(MX[:], SX[:]))
            then1(nc.vector.tensor_tensor(SC[:], EX[:], each(MX[:]), ALU.mult))
            nc.vector.memset(SB[:, :, E1:], MARK)
            then1(nc.vector.tensor_tensor(SB[:, :, 0:E1], SC[:], grow[:, E0:].unsqueeze(1).broadcast_to([P, NT, E1]), ALU.add))
            for t in range(NT):
                last = nc.vector.max(T8[:, t, :], SB[:, t, 0:E1])
            then1(last)
            then1(nc.vector.memset(T8[:, :, K1:], MARK))
            for t in range(NT):
                last = nc.vector.match_replace(out=RP[:, t, :], in_to_replace=T8[:, t, :], in_values=SB[:, t, :],
                                               imm_value=-MARK)
            then1(last)
            then1(nc.vector.tensor_tensor(SEL[:], RP[:, :, 0:E1], SB[:, :, 0:E1], ALU.is_lt))
            then1(nc.vector.tensor_copy(SELh[:], SEL[:]))
            then1(nc.vector.tensor_tensor(WT[:], SEL[:], SC[:], ALU.mult))
            assert chosen[0] == SEL_DONE, chosen
            dve.wait_ge(e1.count_ps, 1)
            nc.vector.tensor_tensor(QS[:], ps[:, 5, 0:NT * E1].rearrange("p (t e) -> p t e", t=NT), SEL[:],
                                    ALU.mult).then_inc(e1.queue, 1)
            dve.wait_ge(e1.z_silu, 1)
            nc.vector.tensor_tensor(ZH[:], ZG[:], ps[0:F1, 2:4, :], ALU.mult).then_inc(e1.z_mult, 1)
            dve.wait_ge(e1.queue, 1)
            dve.wait_ge(ld.late, 80)
            for g in range(8):
                slots = hs[:, G_SLOT + 8 * E1 * g:G_SLOT + 8 * E1 * (g + 1)].rearrange("p (s e) -> p s e", e=E1)
                nc.vector.tensor_tensor(PH[:, :, 8 * g:8 * g + 8], slots.unsqueeze(1).broadcast_to([P, NT, 8, E1]),
                                        QS[:].unsqueeze(2).broadcast_to([P, NT, 8, E1]),
                                        ALU.is_equal).then_inc(e1.onehot, 1)
            def weights(t, p):
                if not known(t) or t >= 2:
                    dve.wait_ge(e1.pw_t, t - 1)
                nc.vector.tensor_tensor(PW[:, p].rearrange("p t (e s) -> p t e s", e=2),
                                        PH[:, :, :, ds(2 * t, 2)].rearrange("p t s e -> p t e s"),
                                        WT[:, :, ds(2 * t, 2)].unsqueeze(3).broadcast_to([P, NT, 2, CAP]),
                                        ALU.mult).then_inc(e1.pw, 1)

            def pair(t, r):
                p = r % 2
                if not known(t) or t < PAIRS - 1:
                    weights(t + 1, 1 - p)
                if not known(t) or t < PAIRS:
                    dve.wait_ge(e1.hidden, t + 1)
                    dve.wait_ge(e1.silu, t + 1)
                    if not known(t) or t >= 2:
                        dve.wait_ge(e1.y, t - 1)
                    nc.vector.tensor_tensor(HG[:, p, :], GG[:, p, :], ps[0:F1, 2 + p, 2 * CAP:4 * CAP],
                                            ALU.mult).then_inc(e1.hg, 1)
            dve.wait_ge(e1.onehot, 8)
            weights(0, 0)
            run_pairs(dve, pair, ahead=1)
            dve.wait_ge(e1.added, PAIRS)
            nc.vector.tensor_tensor(R[:], ps[:, O_BANK, :].rearrange("p (t d) -> p t d", t=NT), X[:],
                                    ALU.add).then_inc(e1.router, 1)
            dve.wait_ge(e1.router, 1)
            norm(9, R, X, EPS_POST)


def kernel(**inputs):
    import concourse.bacc as bacc
    from concourse.bass_utils import run_bass_kernel_spmd

    def a(name):
        return np.asarray(inputs[name])

    def t(name):
        return a(name).T

    consts, halfs = shape_constants()
    zeros = np.zeros
    arrays = {
        "x": a("x").reshape(N, P),
        "ctx": a("ctx_1024").reshape(B * S2, P),
        "mask_x0": a("mask_BxS2_bf1").view(np.uint32).reshape(1, B, S2 // 4),
        "mask_x1": a("mask_BxS2_bk0").view(np.uint32).reshape(1, B, S2 // 4),
        "consts": consts,
        "halfs": halfs,
        "cols": np.stack([a(n) for n in ("L0_xattn_ln1_s", "L0_xattn_ln1_b", "L0_xattn_lnc_s", "L0_xattn_lnc_b",
                                         "L1_attn_bq", "L1_attn_bk", "L1_attn_bv",
                                         "L1_xattn_bq", "L1_xattn_bk", "L1_xattn_bv")], 1),
        "rows": np.stack([a(n) for n in ("L0_xattn_lno_s", "L0_xattn_lno_b", "L1_attn_bo", "L1_xattn_bo")])[None],
        "gate_rows": np.concatenate([a("L0_ffn_balance_bias"), a("L1_ffn_gate_b")])[None],
        "lora": np.stack([a("L0_attn_Bq"), a("L0_attn_Bk"), a("L0_attn_Bv"),
                          t("L0_attn_Aq"), t("L0_attn_Ak"), t("L0_attn_Av")], 1),
        "w_a0": np.stack([t("L0_attn_Wq"), t("L0_attn_Wk"), t("L0_attn_Wv"), t("L0_attn_Wp")], 1),
        "w_x0": np.stack([a("L0_xattn_Wq").reshape(P, XC, P).transpose(1, 0, 2),
                          a("L0_xattn_Wkv")[:, :XC * P].reshape(P, XC, P).transpose(1, 0, 2),
                          a("L0_xattn_Wkv")[:, XC * P:].reshape(P, XC, P).transpose(1, 0, 2)], 2),
        "wq_t_x0": t("L0_xattn_Wq").reshape(XC, P, P).transpose(1, 0, 2),
        "wo_x0": np.concatenate([a("L0_xattn_Wo").reshape(H, XD, P).transpose(1, 0, 2)] * 2),
        "null_kv": np.concatenate([t("L0_xattn_null_kv")] * 2),
        "gate0": t("L0_ffn_gate_w"),
        "w_e0": np.stack([a("L0_ffn_w1").transpose(2, 0, 1),
                          a("L0_ffn_w2").reshape(E0, P, 2, P).transpose(3, 0, 2, 1).reshape(P, E0, F0)], 2),
        "w_a1": np.stack([t("L1_attn_Wq"), t("L1_attn_Wk"), t("L1_attn_Wv"), t("L1_attn_Wo")], 1),
        "w_x1": np.stack([a("L1_xattn_Wq"), a("L1_xattn_Wk"), a("L1_xattn_Wv"), a("L1_xattn_Wo")], 1),
        "gate1": t("L1_ffn_gate_w"),
        "w13_e1": np.stack([a("L1_ffn_w1"), a("L1_ffn_w3")], 1).reshape(E1 // 2, 4, F1, P).transpose(0, 3, 1, 2),
        "w2_e1": a("L1_ffn_w2").reshape(E1 // 2, 2, P, F1).transpose(0, 3, 1, 2),
        "ws13": np.stack([a("L1_ffn_ws1"), a("L1_ffn_ws3")]).reshape(4, F1, P).transpose(2, 0, 1),
        "ws2": a("L1_ffn_ws2").reshape(P, 2, F1).transpose(2, 1, 0),
    }
    nc = bacc.Bacc("TRN2", target_bir_lowering=False, num_devices=1)
    args = []
    for name, v in arrays.items():
        arrays[name] = v = np.ascontiguousarray(v)
        args.append(nc.dram_tensor(f"in_{name}", v.shape, mybir.dt.from_np(v.dtype), kind="ExternalInput").ap())
    result = nc.dram_tensor("out_0", (N, P), F32, kind="ExternalOutput").ap()
    decoder(nc, *args, result)
    r = run_bass_kernel_spmd(nc, [{f"in_{k}": v for k, v in arrays.items()}], core_ids=[0])
    return np.asarray(r.results[0]["out_0"]).reshape(B, T, P)
```
